# Optimizing a Trainium2 kernel written in Bass

```python
import numpy as np
import jax
import jax.numpy as jnp

def _softmax(x, axis=-1):
    return jax.nn.softmax(x, axis=axis)

def _gelu(x):
    return jax.nn.gelu(x, approximate=True)

def _silu(x):
    return jax.nn.silu(x)

def _sigmoid(x):
    return jax.nn.sigmoid(x)

def _layernorm(x, axis=-1, eps=1e-05):
    m = jnp.mean(x, axis=axis, keepdims=True)
    v = jnp.var(x, axis=axis, keepdims=True)
    return (x - m) / jnp.sqrt(v + eps)

def _scatter_add(tgt, idx, src, axis=0):
    return tgt.at[idx].add(src)

def _segment_sum(src, seg, n):
    return jax.ops.segment_sum(src, seg, n)
kernel_name = 'mk_flamingo_gated_d1_seqx_r8_66fdba'

def setup_inputs(seed: int=0):
    np.random.seed(seed)
    _w = jnp.asarray

    def _rec_inputs():
        import jax
        import jax.numpy as jnp
        _rk = jax.random.key(seed)
        x = -0.0003929 + 0.9999 * jax.random.normal(jax.random.fold_in(_rk, 1), (8, 128, 512), jnp.float32)
        _lenS = 128 - jax.random.randint(jax.random.fold_in(_rk, 7), (8,), 0, max(1, 128 // 4) + 1, jnp.int32)
        _lenS2 = 128 - jax.random.randint(jax.random.fold_in(_rk, 8), (8,), 0, max(1, 128 // 4) + 1, jnp.int32)
        _ctx_4096P = jax.random.normal(jax.random.fold_in(_rk, 11), (8, 16, 512), jnp.float32)
        _ctx_4096c = jax.random.dirichlet(jax.random.fold_in(_rk, 511), 0.3 * jnp.ones((16,), jnp.float32), (8, 128))
        _ctx_4096t = jnp.einsum('bsk,bkd->bsd', _ctx_4096c, _ctx_4096P)
        _ctx_4096t = _ctx_4096t * jax.lax.rsqrt(jnp.mean(jnp.square(_ctx_4096t)) + 1e-12) * 0.953939
        ctx_4096 = 2.81802e-05 + 1.00001 * (_ctx_4096t + 0.3 * jax.random.normal(jax.random.fold_in(_rk, 611), (8, 128, 512), jnp.float32))
        pos_BxS2 = jnp.broadcast_to(jnp.arange(128, dtype=jnp.int32), (8, 128))
        _validS = jnp.arange(128)[None, :] < _lenS[:, None]
        _validS2 = jnp.arange(128)[None, :] < _lenS2[:, None]
        _causal = jnp.tril(jnp.ones((128, 128), dtype=bool))
        mask_BxSxS2_ik0 = jnp.where(jnp.broadcast_to(_validS2[:, None, :], (8, 128, 128)), 0, 1).astype(jnp.int32)
        _g = jax.random.normal(jax.random.fold_in(_rk, 9001), (2, 1), jnp.float32)
        _g = jnp.sign(_g) * jnp.maximum(jnp.abs(_g), 1.0) + (_g == 0) * 1.0
        g_xattn = _g[0]
        g_ffn = _g[1]
        return (x, ctx_4096, pos_BxS2, mask_BxSxS2_ik0, g_xattn, g_ffn)
    x, ctx_4096, pos_BxS2, mask_BxSxS2_ik0, g_xattn, g_ffn = _rec_inputs()

    def _L0_xattn_setup():
        import jax, jax.numpy as jnp
        import numpy as np
        B, S, E = (2, 256, 512)
        H, KVH, D = (32, 8, 128)
        GROUPS = H // KVH
        MAX_POS = 512
        ROPE_THETA = 10000.0

        def _rope_tables(max_pos, dim, theta):
            inv_freq = 1.0 / theta ** (jnp.arange(0, dim, 2, dtype=jnp.float32) / dim)
            t = jnp.arange(max_pos, dtype=jnp.float32)
            freqs = jnp.einsum('i,j->ij', t, inv_freq)
            emb = jnp.concatenate([freqs, freqs], axis=-1)
            return (jnp.cos(emb), jnp.sin(emb))

        def _rotate_half(x):
            x1, x2 = (x[..., :x.shape[-1] // 2], x[..., x.shape[-1] // 2:])
            return jnp.concatenate([-x2, x1], axis=-1)
        key = jax.random.key(seed)
        ks = jax.random.split(key, 8)
        scale_w = 1.0 / np.sqrt(E)
        query = jax.random.normal(ks[0], (B, S, E), dtype=jnp.float32)
        k_in = jax.random.normal(ks[1], (B, S, E), dtype=jnp.float32)
        v_in = jax.random.normal(ks[2], (B, S, E), dtype=jnp.float32)
        position_ids = jnp.broadcast_to(jnp.arange(S, dtype=jnp.int64), (B, S))
        src_mask = jnp.tril(jnp.ones((S, S), dtype=jnp.int32))
        src_mask = jnp.broadcast_to(src_mask, (B, S, S))
        Wq = jax.random.normal(ks[3], (E, H * D), dtype=jnp.float32) * scale_w
        Wk = jax.random.normal(ks[4], (E, KVH * D), dtype=jnp.float32) * scale_w
        Wv = jax.random.normal(ks[5], (E, KVH * D), dtype=jnp.float32) * scale_w
        Wo = jax.random.normal(ks[6], (H * D, E), dtype=jnp.float32) * scale_w
        return {'query': query, 'key': k_in, 'value': v_in, 'position_ids': position_ids, 'src_mask': src_mask, 'Wq': Wq, 'Wk': Wk, 'Wv': Wv, 'Wo': Wo}
    _L0_xattn_all = _L0_xattn_setup()
    _L0_xattn_in = {k: v for k, v in _L0_xattn_all.items() if k in ('Wq', 'Wk', 'Wv', 'Wo')}
    del _L0_xattn_all

    def _L0_ffn_setup():
        import jax, jax.numpy as jnp
        import numpy as np
        M = 512
        K = 512

        def _make_2to4_mask(key, shape):
            scores = jax.random.normal(key, shape)
            g = scores.reshape(shape[0], shape[1] // 4, 4)
            rank = jnp.argsort(jnp.argsort(-jnp.abs(g), axis=-1), axis=-1)
            return (rank < 2).reshape(shape).astype(jnp.float32)
        key = jax.random.key(seed)
        k_x, k_w12, k_b12, k_w3, k_b3, k_m = jax.random.split(key, 6)
        x = jax.random.normal(k_x, (4, 256, K), dtype=jnp.float32)
        w12_dense = jax.random.normal(k_w12, (2 * M, K), dtype=jnp.float32) * (1.0 / np.sqrt(K))
        mask12 = _make_2to4_mask(k_m, (2 * M, K))
        w12 = w12_dense * mask12
        b12 = jax.random.normal(k_b12, (2 * M,), dtype=jnp.float32) * 0.01
        w3 = jax.random.normal(k_w3, (M, M), dtype=jnp.float32) * (1.0 / np.sqrt(M))
        b3 = jax.random.normal(k_b3, (M,), dtype=jnp.float32) * 0.01
        return {'x': x, 'w12': w12, 'b12': b12, 'w3': w3, 'b3': b3}
    _L0_ffn_all = _L0_ffn_setup()
    _L0_ffn_in = {k: v for k, v in _L0_ffn_all.items() if k in ('w12', 'b12', 'w3', 'b3')}
    del _L0_ffn_all
    return {'x': x, 'ctx_4096': ctx_4096, 'pos_BxS2': pos_BxS2, 'mask_BxSxS2_ik0': mask_BxSxS2_ik0, 'g_xattn': g_xattn, 'g_ffn': g_ffn, 'L0_xattn_Wq': _L0_xattn_in['Wq'], 'L0_xattn_Wk': _L0_xattn_in['Wk'], 'L0_xattn_Wv': _L0_xattn_in['Wv'], 'L0_xattn_Wo': _L0_xattn_in['Wo'], 'L0_ffn_w12': _L0_ffn_in['w12'], 'L0_ffn_b12': _L0_ffn_in['b12'], 'L0_ffn_w3': _L0_ffn_in['w3'], 'L0_ffn_b3': _L0_ffn_in['b3']}

def reference(x, ctx_4096, pos_BxS2, mask_BxSxS2_ik0, g_xattn, g_ffn, L0_xattn_Wq, L0_xattn_Wk, L0_xattn_Wv, L0_xattn_Wo, L0_ffn_w12, L0_ffn_b12, L0_ffn_w3, L0_ffn_b3):
    import jax
    import jax.numpy as jnp

    def _L0_xattn_ref(query, key, value, position_ids, src_mask, Wq, Wk, Wv, Wo):
        import jax, jax.numpy as jnp
        import numpy as np
        B, S, E = (2, 256, 512)
        H, KVH, D = (32, 8, 128)
        GROUPS = H // KVH
        MAX_POS = 512
        ROPE_THETA = 10000.0

        def _rope_tables(max_pos, dim, theta):
            inv_freq = 1.0 / theta ** (jnp.arange(0, dim, 2, dtype=jnp.float32) / dim)
            t = jnp.arange(max_pos, dtype=jnp.float32)
            freqs = jnp.einsum('i,j->ij', t, inv_freq)
            emb = jnp.concatenate([freqs, freqs], axis=-1)
            return (jnp.cos(emb), jnp.sin(emb))

        def _rotate_half(x):
            x1, x2 = (x[..., :x.shape[-1] // 2], x[..., x.shape[-1] // 2:])
            return jnp.concatenate([-x2, x1], axis=-1)
        nb, q_len, _ = query.shape
        q = (query @ Wq).reshape(nb, q_len, H, D).transpose(0, 2, 1, 3)
        k = (key @ Wk).reshape(nb, q_len, KVH, D).transpose(0, 2, 1, 3)
        v = (value @ Wv).reshape(nb, q_len, KVH, D).transpose(0, 2, 1, 3)
        cos_t, sin_t = _rope_tables(MAX_POS, D, ROPE_THETA)
        cos = cos_t[position_ids][:, None]
        sin = sin_t[position_ids][:, None]
        q = q * cos + _rotate_half(q) * sin
        k = k * cos + _rotate_half(k) * sin
        k = jnp.repeat(k, GROUPS, axis=1)
        v = jnp.repeat(v, GROUPS, axis=1)
        scores = jnp.einsum('bhqd,bhkd->bhqk', q, k) / jnp.sqrt(jnp.float32(D))
        mask = src_mask[:, None]
        scores = jnp.where(mask == 0, jnp.float32(-1000000000.0), scores)
        attn = jax.nn.softmax(scores, axis=-1)
        x = jnp.einsum('bhqk,bhkd->bhqd', attn, v)
        x = x.transpose(0, 2, 1, 3).reshape(nb, q_len, H * D)
        return x @ Wo

    def _L0_ffn_ref(x, w12, b12, w3, b3):
        import jax, jax.numpy as jnp
        import numpy as np
        M = 512
        K = 512

        def _make_2to4_mask(key, shape):
            scores = jax.random.normal(key, shape)
            g = scores.reshape(shape[0], shape[1] // 4, 4)
            rank = jnp.argsort(jnp.argsort(-jnp.abs(g), axis=-1), axis=-1)
            return (rank < 2).reshape(shape).astype(jnp.float32)
        x12 = jnp.einsum('bsk,mk->bsm', x, w12) + b12
        x1, x2 = jnp.split(x12, 2, axis=-1)
        x4 = jax.nn.silu(x1) * x2
        return jnp.einsum('bsm,nm->bsn', x4, w3) + b3
    x = x + jnp.tanh(g_xattn[0]) * _L0_xattn_ref(_layernorm(x, axis=-1), ctx_4096, ctx_4096, pos_BxS2, mask_BxSxS2_ik0, L0_xattn_Wq, L0_xattn_Wk, L0_xattn_Wv, L0_xattn_Wo)
    x = x + jnp.tanh(g_ffn[0]) * _L0_ffn_ref(_layernorm(x, axis=-1), L0_ffn_w12, L0_ffn_b12, L0_ffn_w3, L0_ffn_b3)
    return x

_drawn_inputs = setup_inputs


def setup_inputs(seed=0):
    import zlib

    import numpy as np

    out = dict(_drawn_inputs(seed))
    spreads = {}
    factors = {'L0_ffn_b12': 8.0, 'L0_ffn_b3': 8.0}
    for name, (base, spread) in spreads.items():
        noise = np.random.default_rng([zlib.crc32(name.encode()), seed]).standard_normal(out[name].shape)
        drawn = base * np.exp(spread * noise) if base else spread * noise
        out[name] = jnp.asarray(drawn.astype(out[name].dtype))
    for name, factor in factors.items():
        out[name] = (out[name] * factor).astype(out[name].dtype)
    return out
```

```python
import concourse.bass as bass
import numpy as np
from concourse import mybir
from contextlib import ExitStack

F32 = mybir.dt.float32
F32R = mybir.dt.float32r
I32 = mybir.dt.int32
ALU = mybir.AluOpType
ACT = mybir.ActivationFunctionType

B, S, E = 8, 128, 512
H, KVH, D = 32, 8, 128
GH = H // KVH
KT = E // 128
TOK = B * S
HB = B // 2
HT = HB * S
M = 512
MAX_POS, THETA = 512, 10000.0
EPS = 1e-5
SCORE_SCALE = -1.0 / float(np.sqrt(np.float32(D)))
MASKED = 1e9
KEEP = -float(2.0 ** 126)

UNITS = 2 * KVH
BLOCKS = 6 * UNITS
AHEAD = 7
PAIRS = 2 * UNITS
RAW = 5
W_FIRST, W_GROUP = 6, 10


def rope_table():
    inv_freq = (1.0 / THETA ** (np.arange(0, D, 2, dtype=np.float32) / np.float32(D))).astype(np.float32)
    angle = np.arange(MAX_POS, dtype=np.float32)[:, None] * inv_freq[None, :]
    c, s = np.cos(angle), np.sin(angle)
    return np.ascontiguousarray(np.concatenate([c, c, s, -s], axis=1).astype(np.float32))


def block_of(f):
    return f % 6


def ropes_until(u2, j):
    return 5 * u2 + (1 if j == 0 else j)


def build(nc, x, ctx, pos, mask, g_x, g_f, Wq, Wk, Wv, Wo, w12, b12, w3, b3, out):
    table = nc.inline_tensor(rope_table(), "rope_table")
    table = table.ap() if hasattr(table, "ap") else table
    es = ExitStack()
    base = (nc.sbuf_base + 31) // 32 * 32
    at = {"top": base}

    def place(name, shape, dt, offset=None):
        size = int(np.prod(shape[1:])) * 4
        if offset is None:
            offset = at["top"]
            at["top"] += (size + 31) // 32 * 32
        at[name] = offset
        return nc.alloc_sbuf_tensor_at(name, shape, dt, offset=offset)

    def sem(name):
        return es.enter_context(nc.semaphore(name))

    with es:
        xT_hi, xT_lo = place("xT_hi", [128, KT, TOK], F32R), place("xT_lo", [128, KT, TOK], F32R)
        cT_hi, cT_lo = place("cT_hi", [128, KT, TOK], F32R), place("cT_lo", [128, KT, TOK], F32R)
        resid = place("resid", [128, B, E], F32)
        wq_hi, wq_lo = place("wq_hi", [128, GH, KT * 128], F32R), place("wq_lo", [128, GH, KT * 128], F32R)
        wk_hi, wk_lo = place("wk_hi", [128, KT * 128], F32R), place("wk_lo", [128, KT * 128], F32R)
        wv_hi, wv_lo = place("wv_hi", [128, KT * 128], F32R), place("wv_lo", [128, KT * 128], F32R)
        wo_hi, wo_lo = place("wo_hi", [128, GH, E], F32R), place("wo_lo", [128, GH, E], F32R)
        raw = place("raw", [128, RAW, 512], F32)
        cosT, sinT = place("cosT", [128, TOK], F32), place("sinT", [128, TOK], F32)
        mfill = place("mfill", [128, B, S], F32)
        q32 = place("q32", [128, 2, GH, HT], F32)
        q_hi, q_lo = place("q_hi", [128, 2, GH, S], F32R), place("q_lo", [128, 2, GH, S], F32R)
        k_hi, k_lo = place("k_hi", [128, 2, HT], F32R), place("k_lo", [128, 2, HT], F32R)
        v_hi, v_lo = place("v_hi", [128, 2, HB, D], F32R), place("v_lo", [128, 2, HB, D], F32R)
        k32, v32 = place("k32", [128, HT], F32), place("v32", [128, HT], F32)
        t_cos, t_sin = place("t_cos", [128, 2, HT], F32), place("t_sin", [128, 2, HT], F32)
        prob = place("prob", [128, 2, GH, S], F32)
        pT_hi, pT_lo = place("pT_hi", [128, 2, GH, S], F32R), place("pT_lo", [128, 2, GH, S], F32R)
        o_hi, o_lo = place("o_hi", [128, 2, GH, S], F32R), place("o_lo", [128, 2, GH, S], F32R)
        ident = place("ident", [128, 128], F32)
        small = place("small", [128, 128], F32)
        ctx_raw = place("ctx_raw", [128, B, E], F32, at["q32"])
        rope_tok = place("rope_tok", [128, B, 256], F32, at["k_hi"])
        mask_raw = place("mask_raw", [128, B, S], I32, at["o_hi"])
        ffn_raw = place("ffn_raw", [128, 4, 512], F32, at["wk_hi"])
        act1_hi = place("act1_hi", [128, 4, HT], F32R, at["q32"])
        act1_lo = place("act1_lo", [128, 4, HT], F32R, at["q32"] + 4 * HT * 4)
        b3_row = place("b3_row", [128, E], F32, at["k32"])
        pos_raw = place("pos_raw", [128, B], I32)
        pos_fix = place("pos_fix", [128, B], I32)
        b12_col = place("b12_col", [128, 8], F32)

        def col(i, n=1):
            return small[:, i:i + n]
        nmin = [small[:, 0:4], small[:, 4:8]]
        psum_row = [small[:, 8:12], small[:, 12:16]]
        rrow = [small[:, 16:20], small[:, 20:24]]
        tg_x, tg_f = col(24), col(25)
        graw = col(26, 2)
        mv = small[:, 32:48].rearrange("p (b t) -> p b t", t=2)
        std = col(48, 8)
        rstd = col(56, 8)
        posf = col(64, 8)
        stats = small[:, 72:78]

        banks = [es.enter_context(nc.psum_tensor(f"bank{i}", [128, 512], F32)) for i in range(8)]
        f_bank, s_bank, t_bank, pv_bank, o_bank = banks[0:2], banks[2:4], banks[4], banks[5], banks[6:8]

        x_loaded = [sem(f"x_loaded{i}") for i in range(2)]
        ctx_loaded = [sem(f"ctx_loaded{i}") for i in range(2)]
        pos_loaded, mask_loaded, gate_loaded, bias_loaded = sem("pos_loaded"), sem("mask_loaded"), sem("gate_loaded"), sem("bias_loaded")
        rope_loaded = [sem(f"rope_loaded{i}") for i in range(B)]
        raw_loaded = [sem(f"raw_loaded{i}") for i in range(RAW)]
        ffn_loaded = [sem(f"ffn_loaded{i}") for i in range(4)]
        out_stored = sem("out_stored")
        ident_zero, ident_done = sem("ident_zero"), sem("ident_done")
        dve_small, act_small = sem("dve_small"), sem("act_small")
        dve_xn, pe_tile, act_tile, dve_tile = sem("dve_xn"), sem("pe_tile"), sem("act_tile"), sem("dve_tile")
        pe_block, pe_vT, pe_score, pe_pT, pe_pv, pe_out = (sem(n) for n in ("pe_block", "pe_vT", "pe_score", "pe_pT", "pe_pv", "pe_out"))
        dve_rot, pool_rope, act_khi, pool_klo = (sem(n) for n in ("dve_rot", "pool_rope", "act_khi", "pool_klo"))
        act_v32, act_vhi, dve_vlo = (sem(n) for n in ("act_v32", "act_vhi", "dve_vlo"))
        act_qhi, pool_qlo = sem("act_qhi"), sem("pool_qlo")
        dve_mask, act_exp, dve_recip, pool_norm = (sem(n) for n in ("dve_mask", "act_exp", "dve_recip", "pool_norm"))
        act_pThi, dve_pTlo, act_ohi, dve_olo, dve_acc = (sem(n) for n in ("act_pThi", "dve_pTlo", "act_ohi", "dve_olo", "dve_acc"))
        act_whi, pool_wlo = sem("act_whi"), sem("pool_wlo")
        pe_up, act_silu, dve_gate, act_ghi, dve_glo, pe_down, dve_out, dve_st, dve_b3, bias3_loaded, dve_masked = (sem(n) for n in (
            "pe_up", "act_silu", "dve_gate", "act_ghi", "dve_glo", "pe_down", "dve_out", "dve_st", "dve_b3", "bias3_loaded", "dve_masked"))
        block = es.enter_context(nc.Block())

        def f32(ap):
            return ap.bitcast(F32)

        def last_unit(g, c):
            return isinstance(g, int) and 2 * g + c // 2 == UNITS - 1

        def chunk_src(kind, group):
            if kind == 0 or kind == 1:
                w = Wk if kind == 0 else Wv
                return w[:, bass.ds(group * D, D)].rearrange("(t p) c -> p t c", p=128)
            return Wq[:, bass.ds(group * (GH * D) + (kind - 2) * D, D)].rearrange("(t p) c -> p t c", p=128)

        def wo_src(group, h):
            return Wo[bass.ds(group * (GH * D) + h * D, D), :]

        def chunk_dst(kind):
            if kind == 0:
                return wk_hi[:, :], wk_lo[:, :]
            if kind == 1:
                return wv_hi[:, :], wv_lo[:, :]
            return wq_hi[:, kind - 2, :], wq_lo[:, kind - 2, :]

        def pair_chunks(g, c):
            r, G = c % 4, g + c // 4

            def chunk(off, dst, free):
                return W_GROUP * G + off + 1, off % RAW, 16 * (W_GROUP // RAW * G + off // RAW + 1), dst, free
            if r == 0:
                first = isinstance(G, int) and G == 0
                return [chunk(W_FIRST + h, (wo_hi[:, h, :], wo_lo[:, h, :]), None if first else (pe_out, 8 * G)) for h in range(GH)]
            if isinstance(G, int) and G == KVH - 1:
                return []
            return [chunk(W_GROUP + kind, chunk_dst(kind), (pe_block, 12 * G + 6 + kind + 1)) for kind in {1: [0, 1, 2], 2: [3, 4, 5], 3: []}[r]]

        def rope_slot(idx):
            return (ropes_until(idx // 6, idx % 6) - 1) % 2

        @block.sync
        def _(sp):
            for i in range(2):
                hb = slice(HB * i, HB * (i + 1))
                sp.dma_start(ctx_raw[:, hb, :], ctx[hb].rearrange("b s e -> s b e")).then_inc(ctx_loaded[i], 16)
                sp.dma_start(resid[:, hb, :], x[hb].rearrange("b s e -> s b e")).then_inc(x_loaded[i], 16)
                if i == 0:
                    for s in range(RAW):
                        sp.dma_start(raw[:, s, :].rearrange("p (t c) -> p t c", t=KT), chunk_src(s, 0)).then_inc(raw_loaded[s], 16)

            def load_chunk(s, slot, src, parts):
                sp.wait_ge(act_whi, s - RAW + 1)
                sp.wait_ge(pool_wlo, s - RAW + 1)
                dst = raw[:, slot, :]
                if parts:
                    dst = dst.rearrange("p (t c) -> p t c", t=KT)
                sp.dma_start(dst, src).then_inc(raw_loaded[slot], 16)

            load_chunk(5, 0, chunk_src(5, 0), True)

            def group_loads(G, last):
                s0 = W_FIRST + W_GROUP * G
                for h in range(GH):
                    load_chunk(s0 + h, (W_FIRST + h) % RAW, wo_src(G, h), False)
                if not last:
                    for k in range(6):
                        load_chunk(s0 + 4 + k, (W_FIRST + 4 + k) % RAW, chunk_src(k, G + 1), True)

            with sp.Fori(0, KVH - 1) as G:
                group_loads(G, False)
            group_loads(KVH - 1, True)

            sp.wait_ge(pe_block, BLOCKS - 4)
            for t in range(12):
                if t >= 4:
                    sp.wait_ge(pe_block, BLOCKS + t - 3)
                src = w12[t * 128:(t + 1) * 128, :] if t < 8 else w3[(t - 8) * 128:(t - 7) * 128, :]
                sp.dma_start(ffn_raw[:, t % 4, :], src).then_inc(ffn_loaded[t % 4], 16)
            sp.wait_ge(act_khi, UNITS)
            sp.wait_ge(pool_klo, UNITS)
            sp.dma_start(b3_row[:, :], b3.partition_broadcast(128)).then_inc(bias3_loaded, 16)
            for b in range(B):
                sp.wait_ge(dve_out, b + 1)
                sp.dma_start(out[b], resid[:, b, :]).then_inc(out_stored, 16)
            sp.wait_ge(out_stored, 16 * B)

        @block.tensor
        def _(pe):
            def three(dst, st, mv_, start, stop):
                nc.tensor.matmul(dst, st[0], mv_[0], start=start, stop=False)
                nc.tensor.matmul(dst, st[0], mv_[1], start=False, stop=False)
                return nc.tensor.matmul(dst, st[1], mv_[0], start=False, stop=stop)

            def transpose4(dst, src):
                for t in range(4):
                    mm = nc.tensor.transpose(dst[:, t * 128:(t + 1) * 128], src(t), ident[:, :])
                return mm

            order = [("ctx", b) for b in range(4)] + [("x", b) for b in range(4)] + \
                    [("rope", i) for i in range(4)] + [("ctx", b) for b in range(4, 8)] + [("x", b) for b in range(4, 8)]
            pe.wait_ge(ident_done, 1)
            for t, (what, b) in enumerate(order):
                if t >= 4:
                    pe.wait_ge(act_tile, t - 3)
                    pe.wait_ge(dve_tile, t - 3)
                if what == "ctx":
                    pe.wait_ge(ctx_loaded[b // 4], 16)
                    mm = transpose4(banks[t % 4], lambda k: ctx_raw[:, b, k * 128:(k + 1) * 128])
                elif what == "x":
                    pe.wait_ge(dve_xn, b + 1)
                    mm = transpose4(banks[t % 4], lambda k: prob[:, b % 2].rearrange("p h s -> p (h s)")[:, k * 128:(k + 1) * 128])
                else:
                    pe.wait_ge(rope_loaded[2 * b], 16)
                    pe.wait_ge(rope_loaded[2 * b + 1], 16)
                    mm = transpose4(banks[t % 4], lambda k: rope_tok[:, 2 * b + k % 2, (k // 2) * 128:(k // 2 + 1) * 128])
                mm.then_inc(pe_tile, 1)
            pe.wait_ge(act_tile, len(order))
            pe.wait_ge(dve_tile, len(order))

            def project(kind, half, bank, wready):
                pe.wait_ge(act_whi, wready)
                pe.wait_ge(pool_wlo, wready)
                hi, lo = chunk_dst(kind)
                mh, ml = (cT_hi, cT_lo) if kind < 2 else (xT_hi, xT_lo)
                for k in range(KT):
                    w = slice(k * 128, (k + 1) * 128)
                    tk = slice(half * HT, (half + 1) * HT)
                    mm = three(bank[:, :], (hi[:, w], lo[:, w]), (mh[:, k, tk], ml[:, k, tk]), k == 0, k == KT - 1)
                mm.then_inc(pe_block, 1)

            def bank_free(g, idx):
                p = idx - 2
                u2, j = 2 * g + p // 6, p % 6
                if j == 1:
                    pe.wait_ge(act_v32, u2 + 1)
                else:
                    pe.wait_ge(dve_rot, ropes_until(u2, j))

            for f in range(AHEAD):
                if f >= 2:
                    bank_free(0, f)
                project(f % 6, f // 6, f_bank[f % 2], f % 6 + 1)
                if f == 3:
                    pe.wait_ge(act_v32, 1)
                    transpose4(pv_bank, lambda b: v32[:, b * 128:(b + 1) * 128]).then_inc(pe_vT, 1)

            def block_slot(g, c, i):
                idx = AHEAD + 3 * c + i
                if isinstance(g, int) and 12 * g + idx >= BLOCKS:
                    return
                bank_free(g, idx)
                G = g + idx // 12
                project(idx % 6, (idx // 6) % 2, f_bank[idx % 2], W_GROUP * G + idx % 6 + 1)

            def scores(g, c, k):
                n, sl = 8 * g + 2 * c + k, k
                u2, b = 2 * g + c // 2, 2 * (c % 2) + k
                pe.wait_ge(act_qhi, n + 1)
                pe.wait_ge(pool_qlo, n + 1)
                if k == 0:
                    pe.wait_ge(act_khi, u2 + 1)
                    pe.wait_ge(pool_klo, u2 + 1)
                if not (isinstance(n, int) and n < 2):
                    pe.wait_ge(dve_mask, n - 1)
                ks, bs = (c // 2) % 2, slice(b * S, (b + 1) * S)
                for h in range(GH):
                    mm = three(s_bank[sl][:, h * S:(h + 1) * S], (q_hi[:, sl, h, :], q_lo[:, sl, h, :]),
                               (k_hi[:, ks, bs], k_lo[:, ks, bs]), True, True)
                mm.then_inc(pe_score, 1)

            def prob_transpose(g, c, k):
                n = 8 * g + 2 * c + k
                pe.wait_ge(pool_norm, n + 1)
                pe.wait_ge(act_pThi, n)
                pe.wait_ge(dve_pTlo, n)
                transpose4(t_bank, lambda h: prob[:, k, h, :]).then_inc(pe_pT, 1)

            def pv(g, c, k):
                n = 8 * g + 2 * c + k
                u2, b = 2 * g + c // 2, 2 * (c % 2) + k
                pe.wait_ge(act_pThi, n + 1)
                pe.wait_ge(dve_pTlo, n + 1)
                done = u2 + 1 if last_unit(g, c) else u2 + 2
                pe.wait_ge(act_vhi, done)
                pe.wait_ge(dve_vlo, done)
                pe.wait_ge(act_ohi, n)
                pe.wait_ge(dve_olo, n)
                vs = (c // 2) % 2
                three(pv_bank[:, :], (v_hi[:, vs, b, :], v_lo[:, vs, b, :]),
                      (pT_hi[:, k].rearrange("p h s -> p (h s)"), pT_lo[:, k].rearrange("p h s -> p (h s)")), True, True).then_inc(pe_pv, 1)

            def out_proj(n, k, w_count):
                pe.wait_ge(act_ohi, n + 1)
                pe.wait_ge(dve_olo, n + 1)
                pe.wait_ge(act_whi, w_count)
                pe.wait_ge(pool_wlo, w_count)
                pe.wait_ge(dve_acc, n + 1)
                for h in range(GH):
                    mm = three(o_bank[k][:, :], (o_hi[:, k, h, :], o_lo[:, k, h, :]), (wo_hi[:, h, :], wo_lo[:, h, :]), h == 0, h == GH - 1)
                mm.then_inc(pe_out, 1)

            def pair(g, c):
                first = isinstance(g, int) and 4 * g + c == 0
                u_next = 2 * g + c // 2 + 1
                scores(g, c, 0)
                ffn_or_block(g, c, 0)
                scores(g, c, 1)
                ffn_or_block(g, c, 1)
                if c % 2 == 0 and not last_unit(g, c):
                    if first:
                        pe.wait_ge(act_vhi, 1)
                        pe.wait_ge(dve_vlo, 1)
                    pe.wait_ge(act_v32, u_next + 1)
                    pe.wait_ge(act_ohi, 8 * g + 2 * c)
                    pe.wait_ge(dve_olo, 8 * g + 2 * c)
                    transpose4(pv_bank, lambda b: v32[:, b * 128:(b + 1) * 128]).then_inc(pe_vT, 1)
                Gp = g + (c - 1) // 4
                wcount = W_FIRST + W_GROUP * Gp + GH
                prob_transpose(g, c, 0)
                if not first:
                    out_proj(8 * g + 2 * c - 2, 0, wcount)
                pv(g, c, 0)
                prob_transpose(g, c, 1)
                if not first:
                    out_proj(8 * g + 2 * c - 1, 1, wcount)
                pv(g, c, 1)
                ffn_or_block(g, c, 2)

            ffn_slots = {(1, 2): [0], (2, 0): [1, 2], (2, 1): [3, 4], (2, 2): [5], (3, 0): [6, 7], (3, 1): [8, 9], (3, 2): [10, 11]}

            def ffn_tile(t):
                pe.wait_ge(ffn_loaded[t % 4], 16 * (t // 4 + 1))
                if t < 2:
                    bank_free(KVH - 1, 12 + t)
                else:
                    pe.wait_ge(act_tile, 20 + t - 1)
                    pe.wait_ge(dve_tile, 20 + t - 1)
                transpose4(f_bank[t % 2], lambda k: ffn_raw[:, t % 4, k * 128:(k + 1) * 128]).then_inc(pe_block, 1)

            def ffn_or_block(g, c, i):
                block_slot(g, c, i)
                if isinstance(g, int) and g == KVH - 1:
                    for t in ffn_slots.get((c, i), []):
                        ffn_tile(t)

            pair(0, 0)
            with pe.Fori(0, KVH - 1) as g:
                for c in range(1, 5):
                    pair(g, c)
            for c in range(1, 4):
                pair(KVH - 1, c)

            def h_tile(b):
                pe.wait_ge(dve_xn, B + b + 1)
                pe.wait_ge(act_tile, 32 + b - 1)
                pe.wait_ge(dve_tile, 32 + b - 1)
                transpose4(f_bank[b % 2], lambda k: prob[:, b % 2].rearrange("p h s -> p (h s)")[:, k * 128:(k + 1) * 128]).then_inc(pe_tile, 1)

            n_last = 8 * KVH
            wlast = W_FIRST + W_GROUP * (KVH - 1) + GH
            for b in range(4):
                h_tile(b)
            out_proj(n_last - 2, 0, wlast)
            out_proj(n_last - 1, 1, wlast)
            up_banks = banks[2:6]
            for half in range(2):
                pe.wait_ge(act_tile, 32 + 4 * (half + 1))
                pe.wait_ge(dve_tile, 32 + 4 * (half + 1))
                for m in range(4):
                    i = 4 * half + m
                    if i >= 2:
                        pe.wait_ge(dve_gate, i - 1)
                    for part in range(2):
                        bank = up_banks[2 * (i % 2) + part]
                        for k in range(KT):
                            w = slice((4 * part + m) * 128, (4 * part + m + 1) * 128)
                            tk = slice(half * HT, (half + 1) * HT)
                            mm = three(bank[:, :], (cT_hi[:, k, w], cT_lo[:, k, w]), (xT_hi[:, k, tk], xT_lo[:, k, tk]), k == 0, k == KT - 1)
                    mm.then_inc(pe_up, 1)
                if half == 0:
                    for b in range(4, 8):
                        h_tile(b)
                a_hi, a_lo = (wo_hi, wo_lo) if half == 0 else (act1_hi, act1_lo)
                for b in range(4):
                    n = 4 * half + b
                    pe.wait_ge(act_ghi, 4 * (half + 1))
                    pe.wait_ge(dve_glo, 4 * (half + 1))
                    if n == 0:
                        pe.wait_ge(dve_acc, n_last + 2)
                    if n >= 2:
                        pe.wait_ge(dve_out, n - 1)
                    for m in range(4):
                        ts = slice(b * 128, (b + 1) * 128)
                        mm = three(o_bank[n % 2][:, :], (a_hi[:, m, ts], a_lo[:, m, ts]), (wq_hi[:, m, :], wq_lo[:, m, :]), m == 0, m == 3)
                    mm.then_inc(pe_down, 1)

        def tile_order():
            o = [("ctx", b) for b in range(4)] + [("x", b) for b in range(4)] + [("rope", i) for i in range(4)]
            return o + [("ctx", b) for b in range(4, 8)] + [("x", b) for b in range(4, 8)]

        def w3T(part):
            return (wq_hi, wq_lo)[part]

        def k4(bank):
            return bank[:, :].rearrange("p (k s) -> p k s", k=4)

        @block.scalar
        def _(act):
            act.dma_start(pos_raw[:, :], pos.rearrange("b s -> s b"), allow_slow_non_contiguous=True).then_inc(pos_loaded, 16)
            act.dma_start(graw[:, 0:1], g_x.partition_broadcast(128)).then_inc(gate_loaded, 16)
            act.dma_start(graw[:, 1:2], g_f.partition_broadcast(128)).then_inc(gate_loaded, 16)
            act.dma_start(mask_raw[:, :, :], mask.rearrange("b q k -> q b k")).then_inc(mask_loaded, 16)
            act.dma_start(b12_col[:, :], b12.rearrange("(t p) -> p t", p=128), allow_slow_non_contiguous=True).then_inc(bias_loaded, 16)

            def hi(dst, src, s):
                nc.scalar.activation(dst, src, ACT.Copy).then_inc(s, 1)

            act.wait_ge(gate_loaded, 32)
            nc.scalar.activation(small[:, 24:26], graw, ACT.Tanh).then_inc(act_small, 1)

            def tile_copy(t, what, b, bank):
                act.wait_ge(pe_tile, t + 1)
                if what == "rope":
                    hi(cosT[:, b * 256:(b + 1) * 256], bank[:, 0:256], act_tile)
                else:
                    dst = cT_hi if what == "ctx" else xT_hi
                    hi(dst[:, :, b * 128:(b + 1) * 128], k4(bank), act_tile)

            def split_chunk(done, slot, loaded, dst, free):
                act.wait_ge(raw_loaded[slot], loaded)
                if free is not None:
                    act.wait_ge(*free)
                hi(dst[0], raw[:, slot, :], act_whi)

            tiles = tile_order()
            for t, (what, b) in enumerate(tiles):
                if t == 4:
                    act.wait_ge(dve_small, 4)
                    nc.scalar.activation(std, std, ACT.Sqrt).then_inc(act_small, 1)
                tile_copy(t, what, b, banks[t % 4])
                if t % 3 == 2:
                    s = t // 3
                    if s < W_FIRST:
                        split_chunk(s + 1, s % RAW, 16 * (s // RAW + 1), chunk_dst(s), None)

            def exps(g, c, k):
                n = 8 * g + 2 * c + k
                act.wait_ge(dve_mask, n + 1)
                for h in range(GH):
                    e = nc.scalar.activation(prob[:, k, h, :], prob[:, k, h, :], ACT.Exp, bias=nmin[k][:, h:h + 1],
                                             scale=-1.0, accum_out=psum_row[k][:, h:h + 1])
                e.then_inc(act_exp, 1)

            def v_copy(g, c):
                u2 = 2 * g + c // 2 + 1
                act.wait_ge(pe_block, 6 * u2 + 2)
                act.wait_ge(pe_vT, u2)
                hi(v32[:, :], f_bank[1][:, :], act_v32)

            def v_hi_copy(u2, vs):
                act.wait_ge(pe_vT, u2 + 1)
                if not (isinstance(u2, int) and u2 < 2):
                    act.wait_ge(pe_pv, 4 * u2 - 4)
                hi(v_hi[:, vs], k4(pv_bank), act_vhi)

            def k_hi_copy(u2, ks):
                act.wait_ge(pool_rope, ropes_until(u2, 0))
                if not (isinstance(u2, int) and u2 < 2):
                    act.wait_ge(pe_score, 4 * u2 - 4)
                hi(k_hi[:, ks, :], k32[:, :], act_khi)

            def q_hi_copy(n, u2, qs, k, b):
                act.wait_ge(pool_rope, 5 * u2 + 5)
                if not (isinstance(n, int) and n < 2):
                    act.wait_ge(pe_score, n - 1)
                hi(q_hi[:, k], q32[:, qs, :, b * S:(b + 1) * S], act_qhi)

            def pT_hi_copy(g, c, k):
                n = 8 * g + 2 * c + k
                act.wait_ge(pe_pT, n + 1)
                if not (isinstance(n, int) and n < 2):
                    act.wait_ge(pe_pv, n - 1)
                hi(pT_hi[:, k], k4(t_bank), act_pThi)

            def o_hi_copy(g, c, k):
                n = 8 * g + 2 * c + k
                act.wait_ge(pe_pv, n + 1)
                if not (isinstance(n, int) and n < 2):
                    act.wait_ge(pe_out, n - 1)
                hi(o_hi[:, k], k4(pv_bank), act_ohi)

            act.wait_ge(pe_block, 2)
            hi(v32[:, :], f_bank[1][:, :], act_v32)
            k_hi_copy(0, 0)
            v_hi_copy(0, 0)
            q_hi_copy(0, 0, 0, 0, 0)
            q_hi_copy(1, 0, 0, 1, 1)

            def ffn_tile_copy(t):
                act.wait_ge(pe_block, BLOCKS + t + 1)
                dst = cT_hi[:, :, t * 128:(t + 1) * 128] if t < 8 else wq_hi[:, :, (t - 8) * 128:(t - 7) * 128]
                hi(dst, k4(f_bank[t % 2]), act_tile)

            def pair(g, c):
                fixed = isinstance(g, int)
                P = 4 * g + c
                u2 = 2 * g + c // 2
                more = not (fixed and u2 + 1 >= UNITS)
                chunks = pair_chunks(g, c)
                exps(g, c, 0)
                if c % 2 == 0 and more:
                    v_copy(g, c)
                if c % 4:
                    for ch in chunks[:1]:
                        split_chunk(*ch)
                if fixed and g == KVH - 1:
                    for t in {1: [], 2: [0, 1], 3: [5]}[c]:
                        ffn_tile_copy(t)
                exps(g, c, 1)
                if c % 2 == 0 and more:
                    k_hi_copy(u2 + 1, (c // 2 + 1) % 2)
                    v_hi_copy(u2 + 1, (c // 2 + 1) % 2)
                if fixed and g == KVH - 1:
                    for t in {1: [], 2: [2, 3], 3: [6, 7]}[c]:
                        ffn_tile_copy(t)
                pT_hi_copy(g, c, 0)
                if c % 4:
                    for ch in chunks[1:]:
                        split_chunk(*ch)
                if fixed and g == KVH - 1:
                    for t in {1: [], 2: [4], 3: [8, 9]}[c]:
                        ffn_tile_copy(t)
                o_hi_copy(g, c, 0)
                pT_hi_copy(g, c, 1)
                if not (fixed and P + 1 >= PAIRS):
                    for k in range(2):
                        q_hi_copy(8 * g + 2 * c + 2 + k, 2 * g + (c + 1) // 2, ((c + 1) // 2) % 2, k, 2 * ((c + 1) % 2) + k)
                if c % 4 == 0:
                    for ch in chunks:
                        split_chunk(*ch)
                o_hi_copy(g, c, 1)

            pair(0, 0)
            with act.Fori(0, KVH - 1) as g:
                for c in range(1, 5):
                    pair(g, c)
            for c in range(1, 4):
                pair(KVH - 1, c)
            for t in (10, 11):
                ffn_tile_copy(t)

            def h_copy(b):
                act.wait_ge(pe_tile, 20 + b + 1)
                hi(xT_hi[:, :, b * 128:(b + 1) * 128], k4(f_bank[b % 2]), act_tile)

            act.wait_ge(dve_small, 7)
            nc.scalar.activation(std[:, 0:6], std[:, 0:6], ACT.Sqrt).then_inc(act_small, 1)
            for b in range(4):
                h_copy(b)
            act.wait_ge(dve_small, 9)
            nc.scalar.activation(std[:, 6:8], std[:, 6:8], ACT.Sqrt).then_inc(act_small, 1)
            act.wait_ge(bias_loaded, 16)
            up_banks = banks[2:6]
            for half in range(2):
                a_hi = wo_hi if half == 0 else act1_hi
                for m in range(4):
                    i = 4 * half + m
                    act.wait_ge(pe_up, i + 1)
                    if i >= 2:
                        act.wait_ge(dve_gate, i - 1)
                    nc.scalar.activation(t_cos[:, i % 2, :], up_banks[2 * (i % 2)][:, :], ACT.Silu, bias=b12_col[:, m:m + 1]).then_inc(act_silu, 1)
                    act.wait_ge(dve_gate, i + 1)
                    if i == 0:
                        act.wait_ge(pe_out, 8 * KVH)
                    hi(a_hi[:, m, :], t_sin[:, i % 2, :], act_ghi)
                if half == 0:
                    for b in range(4, 8):
                        h_copy(b)

        @block.gpsimd
        def _(pool):
            pool.memset(ident[:, :], 0.0).then_inc(ident_zero, 1)
            pool.wait_ge(ident_zero, 1)
            pool.affine_select(out=ident[:, :], in_=ident[:, :], compare_op=ALU.not_equal, fill=1.0, base=0,
                               pattern=[[-1, 128]], channel_multiplier=1).then_inc(ident_done, 1)
            pool.wait_ge(dve_small, 3)
            for b in range(B):
                pool.indirect_dma_start(rope_tok[:, b, :], None, table[:, :],
                                        bass.IndirectOffsetOnAxis(ap=pos_fix[:, b:b + 1], axis=0)).then_inc(rope_loaded[b], 16)

            def minus(dst, a, b_, s):
                nc.gpsimd.tensor_tensor(dst, a, b_, ALU.subtract).then_inc(s, 1)

            def split_chunk(done, slot, loaded, dst, free):
                pool.wait_ge(act_whi, done)
                minus(dst[1], raw[:, slot, :], f32(dst[0]), pool_wlo)

            for s in range(W_FIRST):
                split_chunk(s + 1, s % RAW, None, chunk_dst(s), None)

            def rope_add(g, idx):
                u2, j = 2 * g + idx // 6, idx % 6
                cnt = ropes_until(u2, j)
                ts = rope_slot(idx)
                pool.wait_ge(dve_rot, cnt)
                fixed = isinstance(g, int)
                if j == 0:
                    if not (fixed and 12 * g + idx < 6):
                        pool.wait_ge(act_khi, u2)
                        pool.wait_ge(pool_klo, u2)
                    dst = k32[:, :]
                else:
                    if not (fixed and 12 * g + idx < 12):
                        pool.wait_ge(act_qhi, 4 * u2 - 4)
                        pool.wait_ge(pool_qlo, 4 * u2 - 4)
                    dst = q32[:, (idx // 6) % 2, j - 2, :]
                nc.gpsimd.tensor_tensor(dst, t_cos[:, ts, :], t_sin[:, ts, :], ALU.add).then_inc(pool_rope, 1)

            def k_lo_split(u2, ks):
                pool.wait_ge(act_khi, u2 + 1)
                minus(k_lo[:, ks, :], k32[:, :], f32(k_hi[:, ks, :]), pool_klo)

            def q_lo_split(n, qs, k, b):
                pool.wait_ge(act_qhi, n + 1)
                minus(q_lo[:, k], q32[:, qs, :, b * S:(b + 1) * S], f32(q_hi[:, k]), pool_qlo)

            def norm(g, c, k):
                n = 8 * g + 2 * c + k
                pool.wait_ge(dve_recip, n + 1)
                nc.gpsimd.tensor_tensor(prob[:, k], prob[:, k], rrow[k].unsqueeze(2).to_broadcast([128, GH, S]), ALU.mult).then_inc(pool_norm, 1)

            rope_add(0, 0)
            k_lo_split(0, 0)
            for f in range(2, 6):
                rope_add(0, f)
            q_lo_split(0, 0, 0, 0)
            q_lo_split(1, 0, 1, 1)

            def pair(g, c):
                fixed = isinstance(g, int)
                P = 4 * g + c
                u2 = 2 * g + c // 2
                idx = AHEAD + 3 * c

                def exists(i):
                    return not (fixed and 12 * g + i >= BLOCKS)
                chunks = pair_chunks(g, c)
                norm(g, c, 0)
                if exists(idx - 1):
                    rope_add(g, idx - 1)
                if c % 4:
                    for ch in chunks[:1]:
                        split_chunk(*ch)
                if c % 2 and exists(idx):
                    rope_add(g, idx)
                norm(g, c, 1)
                if c % 2 == 0 and exists(idx - 1):
                    k_lo_split(u2 + 1, (c // 2 + 1) % 2)
                if c % 4:
                    for ch in chunks[1:2]:
                        split_chunk(*ch)
                if exists(idx + 1):
                    rope_add(g, idx + 1)
                if c % 4:
                    for ch in chunks[2:]:
                        split_chunk(*ch)
                if not (fixed and P + 1 >= PAIRS):
                    for k in range(2):
                        q_lo_split(8 * g + 2 * c + 2 + k, ((c + 1) // 2) % 2, k, 2 * ((c + 1) % 2) + k)
                if c % 4 == 0:
                    for ch in chunks:
                        split_chunk(*ch)

            pair(0, 0)
            with pool.Fori(0, KVH - 1) as g:
                for c in range(1, 5):
                    pair(g, c)
            for c in range(1, 4):
                pair(KVH - 1, c)

        @block.vector
        def _(dve):
            dve.sem_inc(dve_acc, 2)
            dve.wait_ge(pos_loaded, 16)
            nc.vector.tensor_scalar(posf, pos_raw[:, :], 0.0, float(MAX_POS), ALU.is_lt, ALU.mult).then_inc(dve_small, 1)
            dve.wait_ge(dve_small, 1)
            nc.vector.tensor_tensor(posf, posf, pos_raw[:, :], ALU.add).then_inc(dve_small, 1)
            dve.wait_ge(dve_small, 2)
            nc.vector.tensor_scalar(pos_fix[:, :], posf, 0.0, float(MAX_POS - 1), ALU.max, ALU.min).then_inc(dve_small, 1)

            def lo(dst, src, hi_part, s):
                nc.vector.tensor_tensor(dst, src, f32(hi_part), ALU.subtract).then_inc(s, 1)

            def stats_of(b, s_cnt):
                nc.vector.bn_stats(stats, resid[:, b, :]).then_inc(dve_st, 1)
                dve.wait_ge(dve_st, s_cnt + 1)
                nc.vector.bn_aggr(mv[:, b, :], stats).then_inc(dve_st, 1)
                dve.wait_ge(dve_st, s_cnt + 2)

            for b in range(B):
                dve.wait_ge(x_loaded[b // 4], 16)
                stats_of(b, 2 * b)
            nc.vector.tensor_scalar(std, mv[:, :, 1], EPS, None, ALU.add).then_inc(dve_small, 1)
            dve.wait_ge(mask_loaded, 16)
            nc.vector.tensor_scalar(mfill[:, :, :], mask_raw[:, :, :], 0.0, KEEP, ALU.not_equal, ALU.mult).then_inc(dve_masked, 1)
            dve.wait_ge(dve_masked, 1)
            nc.vector.tensor_scalar(mfill[:, :, :], mfill[:, :, :], MASKED, None, ALU.add).then_inc(dve_small, 1)

            tiles = tile_order()

            def tile_lo(t, what, b, bank):
                dve.wait_ge(act_tile, t + 1)
                if what == "rope":
                    nc.vector.tensor_copy(sinT[:, b * 256:(b + 1) * 256], bank[:, 256:512]).then_inc(dve_tile, 1)
                else:
                    dst, h = (cT_lo, cT_hi) if what == "ctx" else (xT_lo, xT_hi)
                    sl = slice(b * 128, (b + 1) * 128)
                    lo(dst[:, :, sl], k4(bank), h[:, :, sl], dve_tile)

            def normalise(b, reader):
                if b >= 2:
                    dve.wait_ge(pe_tile, reader)
                nc.vector.tensor_scalar(prob[:, b % 2].rearrange("p h s -> p (h s)"), resid[:, b, :], mv[:, b, 0:1], rstd[:, b:b + 1],
                                        ALU.subtract, ALU.mult).then_inc(dve_xn, 1)

            for t in range(4):
                tile_lo(t, *tiles[t], banks[t % 4])
            dve.wait_ge(act_small, 2)
            nc.vector.reciprocal(rstd, std).then_inc(dve_small, 1)
            dve.wait_ge(dve_small, 6)
            normalise(0, 0)
            normalise(1, 0)
            for t in range(4, 20):
                tile_lo(t, *tiles[t], banks[t % 4])
                if tiles[t][0] == "x" and tiles[t][1] + 2 < 4:
                    normalise(tiles[t][1] + 2, t + 1)
                if t == 8 or t == 9:
                    normalise(t - 4, t - 1)
                if tiles[t][0] == "x" and 4 <= tiles[t][1] < 6:
                    normalise(tiles[t][1] + 2, t + 1)

            def rotate(g, idx):
                u2, j, half = 2 * g + idx // 6, idx % 6, (idx // 6) % 2
                fixed = isinstance(g, int)
                bank = f_bank[idx % 2]
                ts = rope_slot(idx)
                f_cnt = 12 * g + idx + 1
                dve.wait_ge(pe_block, f_cnt)
                cnt = ropes_until(u2, j)
                if not (fixed and ropes_until(2 * g + idx // 6, j) <= 2):
                    dve.wait_ge(pool_rope, cnt - 2)
                tk = slice(half * HT, (half + 1) * HT)

                def times(dst, a, b_):
                    if j == 0:
                        return nc.vector.scalar_tensor_tensor(out=dst, in0=a, scalar=SCORE_SCALE, in1=b_, op0=ALU.mult, op1=ALU.mult)
                    return nc.vector.tensor_tensor(dst, a, b_, ALU.mult)
                times(t_cos[:, ts, :], bank[:, :], cosT[:, tk])
                times(t_sin[64:128, ts, :], bank[0:64, :], sinT[0:64, tk])
                times(t_sin[0:64, ts, :], bank[64:128, :], sinT[64:128, tk]).then_inc(dve_rot, 1)

            def v_lo_split(u2, vs):
                dve.wait_ge(act_vhi, u2 + 1)
                lo(v_lo[:, vs], k4(pv_bank), v_hi[:, vs], dve_vlo)

            rotate(0, 0)
            rotate(0, 2)
            v_lo_split(0, 0)
            for f in range(3, 6):
                rotate(0, f)

            def mask_scores(g, c, k):
                n = 8 * g + 2 * c + k
                dve.wait_ge(pe_score, n + 1)
                if not (isinstance(n, int) and n < 2):
                    dve.wait_ge(pe_pT, n - 1)
                b = (2 * c + k) % B
                nc.vector.tensor_tensor(prob[:, k], k4(s_bank[k]), mfill[:, b, :].unsqueeze(1).to_broadcast([128, GH, S]),
                                        ALU.max).then_inc(dve_masked, 1)
                dve.wait_ge(dve_masked, n + 2)
                nc.vector.tensor_reduce(nmin[k], prob[:, k], mybir.AxisListType.X, ALU.min).then_inc(dve_mask, 1)

            def recip(g, c, k):
                dve.wait_ge(act_exp, 8 * g + 2 * c + k + 1)
                nc.vector.reciprocal(rrow[k], psum_row[k]).then_inc(dve_recip, 1)

            def pT_lo_split(g, c, k):
                dve.wait_ge(act_pThi, 8 * g + 2 * c + k + 1)
                lo(pT_lo[:, k], k4(t_bank), pT_hi[:, k], dve_pTlo)

            def o_lo_split(g, c, k):
                dve.wait_ge(act_ohi, 8 * g + 2 * c + k + 1)
                lo(o_lo[:, k], k4(pv_bank), o_hi[:, k], dve_olo)

            def add_out(n, b, k):
                dve.wait_ge(pe_out, n + 1)
                nc.vector.scalar_tensor_tensor(out=resid[:, b, :], in0=o_bank[k][:, :], scalar=tg_x, in1=resid[:, b, :],
                                               op0=ALU.mult, op1=ALU.add).then_inc(dve_acc, 1)

            def ffn_tile_lo(t):
                dve.wait_ge(act_tile, 20 + t + 1)
                if t < 8:
                    dst, h = cT_lo[:, :, t * 128:(t + 1) * 128], cT_hi[:, :, t * 128:(t + 1) * 128]
                else:
                    dst, h = (w[:, :, (t - 8) * 128:(t - 7) * 128] for w in (wq_lo, wq_hi))
                lo(dst, k4(f_bank[t % 2]), h, dve_tile)

            def pair(g, c):
                fixed = isinstance(g, int)
                u2 = 2 * g + c // 2
                idx = AHEAD + 3 * c

                def exists(i):
                    return not (fixed and 12 * g + i >= BLOCKS)
                mask_scores(g, c, 0)
                if exists(idx - 1):
                    rotate(g, idx - 1)
                recip(g, c, 0)
                if fixed and g == KVH - 1:
                    for t in {1: [], 2: [0, 1], 3: [5]}[c]:
                        ffn_tile_lo(t)
                mask_scores(g, c, 1)
                if c % 2 and exists(idx):
                    rotate(g, idx)
                recip(g, c, 1)
                if c % 2 == 0 and not (fixed and u2 + 1 >= UNITS):
                    v_lo_split(u2 + 1, (c // 2 + 1) % 2)
                if fixed and g == KVH - 1:
                    for t in {1: [], 2: [2, 3], 3: [6, 7]}[c]:
                        ffn_tile_lo(t)
                pT_lo_split(g, c, 0)
                if exists(idx + 1):
                    rotate(g, idx + 1)
                if fixed and g == KVH - 1:
                    for t in {1: [], 2: [4], 3: [8, 9]}[c]:
                        ffn_tile_lo(t)
                first = fixed and 4 * g + c == 0
                if not first:
                    add_out(8 * g + 2 * c - 2, (2 * c - 2) % B, 0)
                o_lo_split(g, c, 0)
                pT_lo_split(g, c, 1)
                if not first:
                    add_out(8 * g + 2 * c - 1, (2 * c - 1) % B, 1)
                o_lo_split(g, c, 1)

            dve.wait_ge(act_small, 1)
            pair(0, 0)
            with dve.Fori(0, KVH - 1) as g:
                for c in range(1, 5):
                    pair(g, c)
            for c in range(1, 4):
                pair(KVH - 1, c)
            for t in (10, 11):
                ffn_tile_lo(t)

            dve.wait_ge(dve_acc, 8 * KVH)
            dve.wait_ge(pe_pT, 8 * KVH)
            for b in range(6):
                stats_of(b, 2 * B + 2 * b)
            nc.vector.tensor_scalar(std[:, 0:6], mv[:, 0:6, 1], EPS, None, ALU.add).then_inc(dve_small, 1)
            dve.wait_ge(act_small, 3)
            nc.vector.reciprocal(rstd[:, 0:6], std[:, 0:6]).then_inc(dve_small, 1)
            dve.wait_ge(dve_small, 8)

            def h_lo(b):
                dve.wait_ge(act_tile, 32 + b + 1)
                sl = slice(b * 128, (b + 1) * 128)
                lo(xT_lo[:, :, sl], k4(f_bank[b % 2]), xT_hi[:, :, sl], dve_tile)

            normalise(0, 0)
            normalise(1, 0)
            for b in range(4):
                h_lo(b)
                normalise(b + 2, 20 + b + 1)
            dve.wait_ge(bias3_loaded, 16)
            add_out(8 * KVH - 2, 6, 0)
            add_out(8 * KVH - 1, 7, 1)
            dve.wait_ge(dve_acc, 8 * KVH + 2)
            for b in (6, 7):
                stats_of(b, 2 * B + 2 * b)
            nc.vector.tensor_scalar(std[:, 6:8], mv[:, 6:8, 1], EPS, None, ALU.add).then_inc(dve_small, 1)
            dve.wait_ge(act_small, 4)
            nc.vector.reciprocal(rstd[:, 6:8], std[:, 6:8]).then_inc(dve_small, 1)
            dve.wait_ge(dve_small, 10)

            def add_b3(b):
                nc.vector.scalar_tensor_tensor(out=resid[:, b, :], in0=b3_row[:, :], scalar=tg_f, in1=resid[:, b, :],
                                               op0=ALU.mult, op1=ALU.add).then_inc(dve_b3, 1)

            up_banks = banks[2:6]
            for half in range(2):
                a_hi, a_lo = (wo_hi, wo_lo) if half == 0 else (act1_hi, act1_lo)
                for m in range(4):
                    i = 4 * half + m
                    dve.wait_ge(act_silu, i + 1)
                    if i >= 2:
                        dve.wait_ge(act_ghi, i - 1)
                        dve.wait_ge(dve_glo, i - 1)
                    nc.vector.scalar_tensor_tensor(out=t_sin[:, i % 2, :], in0=up_banks[2 * (i % 2) + 1][:, :], scalar=b12_col[:, 4 + m:5 + m],
                                                   in1=t_cos[:, i % 2, :], op0=ALU.add, op1=ALU.mult).then_inc(dve_gate, 1)
                    dve.wait_ge(act_ghi, i + 1)
                    lo(a_lo[:, m, :], t_sin[:, i % 2, :], a_hi[:, m, :], dve_glo)
                    if half == 0:
                        add_b3(m)
                    else:
                        add_b3(4 + m)
                if half == 0:
                    for b in range(4, 8):
                        h_lo(b)
                        if b < 6:
                            normalise(b + 2, 20 + b + 1)
                for b in range(4):
                    n = 4 * half + b
                    dve.wait_ge(pe_down, n + 1)
                    dve.wait_ge(dve_b3, n + 1)
                    nc.vector.scalar_tensor_tensor(out=resid[:, n, :], in0=o_bank[n % 2][:, :], scalar=tg_f, in1=resid[:, n, :],
                                                   op0=ALU.mult, op1=ALU.add).then_inc(dve_out, 1)


_INS = ['x', 'ctx_4096', 'pos_BxS2', 'mask_BxSxS2_ik0', 'g_xattn', 'g_ffn', 'L0_xattn_Wq', 'L0_xattn_Wk', 'L0_xattn_Wv',
        'L0_xattn_Wo', 'L0_ffn_w12', 'L0_ffn_b12', 'L0_ffn_w3', 'L0_ffn_b3']
_OUTS = [((8, 128, 512), 'float32')]


def kernel(**inputs):
    import numpy as _np
    import concourse.bacc as _bacc
    from concourse import mybir as _mybir
    from concourse.bass_utils import run_bass_kernel_spmd as _run

    nc = _bacc.Bacc("TRN2", target_bir_lowering=False, num_devices=1, dynamic_dma_scratch_size=4096)
    arrays, args = {}, []
    for name in _INS:
        a = _np.ascontiguousarray(inputs[name])
        arrays[f"in_{name}_dram"] = a
        args.append(nc.dram_tensor(f"in_{name}_dram", a.shape, _mybir.dt.from_np(a.dtype), kind="ExternalInput").ap())
    for i, (shape, dtype) in enumerate(_OUTS):
        dt = _mybir.dt.from_np(_np.dtype(dtype))
        args.append(nc.dram_tensor(f"out_{i}_dram", shape, dt, kind="ExternalOutput").ap())
    build(nc, *args)
    r = _run(nc, [arrays], core_ids=[0])
    return r.results[0]["out_0_dram"]
```

```python
import concourse.bass as bass
import numpy as np
from concourse import mybir
from contextlib import ExitStack

F32 = mybir.dt.float32
F32R = mybir.dt.float32r
I32 = mybir.dt.int32
ALU = mybir.AluOpType
ACT = mybir.ActivationFunctionType

B, S, E = 8, 128, 512
H, KVH, D = 32, 8, 128
GH = H // KVH
KT = E // 128
TOK = B * S
HB = B // 2
HT = HB * S
M = 512
MAX_POS, THETA = 512, 10000.0
EPS = 1e-5
SCORE_SCALE = -1.0 / float(np.sqrt(np.float32(D)))
MASKED = float(2.0 ** 100)

NEWTON = 3
NEWTON_OPS = 2 + 3 * NEWTON

UNITS = 2 * KVH
BLOCKS = 6 * UNITS
AHEAD = 7
PAIRS = 2 * UNITS
RAW = 5
W_FIRST, W_GROUP = 6, 10


def rope_table():
    inv_freq = (1.0 / THETA ** (np.arange(0, D, 2, dtype=np.float32) / np.float32(D))).astype(np.float32)
    angle = np.arange(MAX_POS, dtype=np.float32)[:, None] * inv_freq[None, :]
    c, s = np.cos(angle), np.sin(angle)
    return np.ascontiguousarray(np.concatenate([c, c, s, -s], axis=1).astype(np.float32))


def block_of(f):
    return f % 6


def ropes_until(u2, j):
    return 5 * u2 + (1 if j == 0 else j)


def build(nc, x, ctx, pos, mask, g_x, g_f, Wq, Wk, Wv, Wo, w12, b12, w3, b3, out):
    table = nc.inline_tensor(rope_table(), "rope_table")
    table = table.ap() if hasattr(table, "ap") else table
    es = ExitStack()
    base = (nc.sbuf_base + 31) // 32 * 32
    at = {"top": base}

    def place(name, shape, dt, offset=None):
        size = int(np.prod(shape[1:])) * 4
        if offset is None:
            offset = at["top"]
            at["top"] += (size + 31) // 32 * 32
        at[name] = offset
        return nc.alloc_sbuf_tensor_at(name, shape, dt, offset=offset)

    def sem(name):
        return es.enter_context(nc.semaphore(name))

    with es:
        xT_hi, xT_lo = place("xT_hi", [128, KT, TOK], F32R), place("xT_lo", [128, KT, TOK], F32R)
        cT_hi, cT_lo = place("cT_hi", [128, KT, TOK], F32R), place("cT_lo", [128, KT, TOK], F32R)
        resid = place("resid", [128, B, E], F32)
        wq_hi, wq_lo = place("wq_hi", [128, GH, KT * 128], F32R), place("wq_lo", [128, GH, KT * 128], F32R)
        wk_hi, wk_lo = place("wk_hi", [128, KT * 128], F32R), place("wk_lo", [128, KT * 128], F32R)
        wv_hi, wv_lo = place("wv_hi", [128, KT * 128], F32R), place("wv_lo", [128, KT * 128], F32R)
        wo_hi, wo_lo = place("wo_hi", [128, GH, E], F32R), place("wo_lo", [128, GH, E], F32R)
        raw = place("raw", [128, RAW, 512], F32)
        cosT, sinT = place("cosT", [128, TOK], F32), place("sinT", [128, TOK], F32)
        mfill = place("mfill", [128, B, S], F32)
        q32 = place("q32", [128, 2, GH, HT], F32)
        q_hi, q_lo = place("q_hi", [128, 2, GH, S], F32R), place("q_lo", [128, 2, GH, S], F32R)
        k_parts = place("k_parts", [128, 2, HB, 2 * S], F32R)
        v_hi, v_lo = place("v_hi", [128, 2, HB, D], F32R), place("v_lo", [128, 2, HB, D], F32R)
        k32, v32 = place("k32", [128, HT], F32), place("v32", [128, HT], F32)
        t_cos, t_sin = place("t_cos", [128, 2, HT], F32), place("t_sin", [128, 2, HT], F32)
        prob = place("prob", [128, 2, GH, S], F32)
        pT_hi, pT_lo = place("pT_hi", [128, 2, GH, S], F32R), place("pT_lo", [128, 2, GH, S], F32R)
        o_hi, o_lo = place("o_hi", [128, 2, GH, S], F32R), place("o_lo", [128, 2, GH, S], F32R)
        xnorm = place("xnorm", [128, 2, E], F32, at["prob"])
        ident = place("ident", [128, 128], F32)
        small = place("small", [128, 128], F32)
        ctx_raw = place("ctx_raw", [128, B, E], F32, at["q32"])
        rope_tok = place("rope_tok", [128, B, 256], F32, at["pT_hi"])
        mask_raw = place("mask_raw", [128, B, S], I32, at["o_hi"])
        ffn_raw = place("ffn_raw", [128, 4, 512], F32, at["wk_hi"])
        ffn_raw2 = place("ffn_raw2", [128, 4, 512], F32, at["q32"])
        xnorm2 = place("xnorm2", [128, 4, E], F32, at["cosT"])
        act1_hi = place("act1_hi", [128, 4, HT], F32R, at["q32"])
        act1_lo = place("act1_lo", [128, 4, HT], F32R, at["q32"] + 4 * HT * 4)
        b3_row = place("b3_row", [128, E], F32, at["k32"])
        pos_raw = place("pos_raw", [128, B], I32)
        pos_fix = place("pos_fix", [128, B], I32)
        b12_col = place("b12_col", [128, 8], F32)

        def col(i, n=1):
            return small[:, i:i + n]
        nmin = [small[:, 0:4], small[:, 4:8]]
        psum_row = [small[:, 8:12], small[:, 12:16]]
        rrow = [small[:, 16:20], small[:, 20:24]]
        tg_x, tg_f = col(24), col(25)
        graw = col(26, 2)
        mv = small[:, 32:48].rearrange("p (b t) -> p b t", t=2)
        var = col(48, 8)
        rstd = col(56, 8)
        newton = col(80, 8)
        posf = col(64, 8)
        stats = small[:, 72:78]

        def bank(name, n=1):
            return es.enter_context(nc.psum_tensor(name, [128, 512 * n], F32))
        f_bank = [bank("f_bank0"), bank("f_bank1")]
        s_banks, t_bank, pv_bank = bank("s_banks", 2), bank("t_bank"), bank("pv_bank")
        o_bank = [bank("o_bank0"), bank("o_bank1")]
        s_parts = s_banks[:, :].rearrange("p (h two k) -> p h two k", h=GH, two=2)
        tile_bank = [s_banks[:, 0:512], s_banks[:, 512:1024], o_bank[0][:, :], o_bank[1][:, :]]
        up_bank = [s_banks[:, 0:512], s_banks[:, 512:1024], t_bank[:, :], pv_bank[:, :]]

        x_loaded = [sem(f"x_loaded{i}") for i in range(B)]
        ctx_loaded = [sem(f"ctx_loaded{i}") for i in range(B)]
        pos_loaded, mask_loaded, gate_loaded, bias_loaded = sem("pos_loaded"), sem("mask_loaded"), sem("gate_loaded"), sem("bias_loaded")
        rope_loaded = [sem(f"rope_loaded{i}") for i in range(B)]
        raw_loaded = [sem(f"raw_loaded{i}") for i in range(RAW)]
        ffn_loaded = [sem(f"ffn_loaded{i}") for i in range(7)]
        out_stored = sem("out_stored")
        ident_zero, ident_done = sem("ident_zero"), sem("ident_done")
        dve_small, act_small = sem("dve_small"), sem("act_small")
        dve_xn, pe_tile, act_tile, dve_tile = sem("dve_xn"), sem("pe_tile"), sem("act_tile"), sem("dve_tile")
        pe_block, pe_vT, pe_score, pe_pT, pe_pv, pe_out = (sem(n) for n in ("pe_block", "pe_vT", "pe_score", "pe_pT", "pe_pv", "pe_out"))
        dve_rot, pool_rope, act_khi, pool_klo = (sem(n) for n in ("dve_rot", "pool_rope", "act_khi", "pool_klo"))
        act_v32, act_vhi, dve_vlo = (sem(n) for n in ("act_v32", "act_vhi", "dve_vlo"))
        act_qhi, pool_qlo = sem("act_qhi"), sem("pool_qlo")
        dve_mask, act_exp, dve_recip, pool_norm = (sem(n) for n in ("dve_mask", "act_exp", "dve_recip", "pool_norm"))
        act_pThi, dve_pTlo, act_ohi, dve_olo, dve_acc = (sem(n) for n in ("act_pThi", "dve_pTlo", "act_ohi", "dve_olo", "dve_acc"))
        act_whi, pool_wlo = sem("act_whi"), sem("pool_wlo")
        pe_up, act_silu, dve_gate, act_ghi, dve_glo, pe_down, dve_out, dve_st, dve_b3, bias3_loaded, dve_masked = (sem(n) for n in (
            "pe_up", "act_silu", "dve_gate", "act_ghi", "dve_glo", "pe_down", "dve_out", "dve_st", "dve_b3", "bias3_loaded", "dve_masked"))
        dve_newton = sem("dve_newton")
        block = es.enter_context(nc.Block())

        def f32(ap):
            return ap.bitcast(F32)

        def last_unit(g, c):
            return isinstance(g, int) and 2 * g + c // 2 == UNITS - 1

        def chunk_src(kind, group):
            if kind == 0 or kind == 1:
                w = Wk if kind == 0 else Wv
                return w[:, bass.ds(group * D, D)].rearrange("(t p) c -> p t c", p=128)
            return Wq[:, bass.ds(group * (GH * D) + (kind - 2) * D, D)].rearrange("(t p) c -> p t c", p=128)

        def wo_src(group, h):
            return Wo[bass.ds(group * (GH * D) + h * D, D), :]

        def chunk_dst(kind):
            if kind == 0:
                return wk_hi[:, :], wk_lo[:, :]
            if kind == 1:
                return wv_hi[:, :], wv_lo[:, :]
            return wq_hi[:, kind - 2, :], wq_lo[:, kind - 2, :]

        def pair_chunks(g, c):
            r, G = c % 4, g + c // 4

            def chunk(off, dst, free):
                return W_GROUP * G + off + 1, off % RAW, 16 * (W_GROUP // RAW * G + off // RAW + 1), dst, free
            if r == 0:
                first = isinstance(G, int) and G == 0
                return [chunk(W_FIRST + h, (wo_hi[:, h, :], wo_lo[:, h, :]), None if first else (pe_out, 8 * G)) for h in range(GH)]
            if isinstance(G, int) and G == KVH - 1:
                return []
            return [chunk(W_GROUP + kind, chunk_dst(kind), (pe_block, 12 * G + 6 + kind + 1)) for kind in {1: [0, 1, 2], 2: [3, 4, 5], 3: []}[r]]

        def rope_slot(idx):
            return (ropes_until(idx // 6, idx % 6) - 1) % 2

        TILES = [("ctx", b) for b in range(4)] + [("rope", 0), ("rope", 1)] + [("x", b) for b in range(4)] + \
                [("ctx", b) for b in range(4, 8)] + [("x", b) for b in range(4, 8)] + [("rope", 2), ("rope", 3)]
        FFN_T = len(TILES)
        H_T = FFN_T + 12

        def tile_of(what, b):
            return TILES.index((what, b))

        def ffn_tile_src(t):
            if t < RAW:
                return raw[:, t, :], raw_loaded[t], 16 * ((W_FIRST + W_GROUP * KVH - 6 + t) // RAW + 1)
            if t < RAW + 4:
                return ffn_raw[:, t - RAW, :], ffn_loaded[t - RAW], 16
            return ffn_raw2[:, t - RAW - 4, :], ffn_loaded[t - RAW], 16

        @block.sync
        def _(sp):
            def rows(dst, src, b, s):
                sp.dma_start(dst[:, b, :], src[b]).then_inc(s[b], 16)

            def first_chunk(s):
                sp.dma_start(raw[:, s, :].rearrange("p (t c) -> p t c", t=KT), chunk_src(s, 0)).then_inc(raw_loaded[s], 16)
            for b in range(4):
                rows(ctx_raw, ctx, b, ctx_loaded)
            first_chunk(0)
            first_chunk(1)
            for b in range(4):
                rows(resid, x, b, x_loaded)
            for s in range(2, RAW):
                first_chunk(s)
            for b in range(4, 8):
                rows(ctx_raw, ctx, b, ctx_loaded)
            for b in range(4, 8):
                rows(resid, x, b, x_loaded)
            sp.dma_start(mask_raw[:, :, :], mask.rearrange("b q k -> q b k")).then_inc(mask_loaded, 16)

            def load_chunk(s, slot, src, parts):
                sp.wait_ge(act_whi, s - RAW + 1)
                sp.wait_ge(pool_wlo, s - RAW + 1)
                dst = raw[:, slot, :]
                if parts:
                    dst = dst.rearrange("p (t c) -> p t c", t=KT)
                sp.dma_start(dst, src).then_inc(raw_loaded[slot], 16)

            load_chunk(5, 0, chunk_src(5, 0), True)

            def group_loads(G, last):
                s0 = W_FIRST + W_GROUP * G
                for h in range(GH):
                    load_chunk(s0 + h, (W_FIRST + h) % RAW, wo_src(G, h), False)
                if not last:
                    for k in range(6):
                        load_chunk(s0 + 4 + k, (W_FIRST + 4 + k) % RAW, chunk_src(k, G + 1), True)

            with sp.Fori(0, KVH - 1) as G:
                group_loads(G, False)
            group_loads(KVH - 1, True)

            for t in range(12):
                dst, s, _ = ffn_tile_src(t)
                if t < RAW:
                    sp.wait_ge(act_whi, W_FIRST + W_GROUP * KVH - 6 + t - RAW + 1)
                    sp.wait_ge(pool_wlo, W_FIRST + W_GROUP * KVH - 6 + t - RAW + 1)
                elif t == RAW:
                    sp.wait_ge(pe_block, BLOCKS - 4)
                elif t == RAW + 4:
                    sp.wait_ge(act_qhi, 4 * (UNITS - 1))
                    sp.wait_ge(pool_qlo, 4 * (UNITS - 1))
                src = w12[t * 128:(t + 1) * 128, :] if t < 8 else w3[(t - 8) * 128:(t - 7) * 128, :]
                sp.dma_start(dst, src).then_inc(s, 16)
            sp.wait_ge(act_khi, UNITS)
            sp.wait_ge(pool_klo, UNITS)
            sp.dma_start(b3_row[:, :], b3.partition_broadcast(128)).then_inc(bias3_loaded, 16)
            for b in range(B):
                sp.wait_ge(dve_out, b + 1)
                sp.dma_start(out[b], resid[:, b, :]).then_inc(out_stored, 16)
            sp.wait_ge(out_stored, 16 * B)

        @block.tensor
        def _(pe):
            def three(dst, st, mv_, start, stop):
                nc.tensor.matmul(dst, st[0], mv_[0], start=start, stop=False)
                nc.tensor.matmul(dst, st[0], mv_[1], start=False, stop=False)
                return nc.tensor.matmul(dst, st[1], mv_[0], start=False, stop=stop)

            def transpose4(dst, src):
                for t in range(4):
                    mm = nc.tensor.transpose(dst[:, t * 128:(t + 1) * 128], src(t), ident[:, :])
                return mm

            def tile(what, b):
                t = tile_of(what, b)
                if t >= 4:
                    pe.wait_ge(act_tile, t - 3)
                    pe.wait_ge(dve_tile, t - 3)
                if what == "ctx":
                    pe.wait_ge(ctx_loaded[b], 16)
                    mm = transpose4(tile_bank[t % 4], lambda k: ctx_raw[:, b, k * 128:(k + 1) * 128])
                elif what == "x":
                    pe.wait_ge(dve_xn, b + 1)
                    mm = transpose4(tile_bank[t % 4], lambda k: xnorm[:, b % 2, k * 128:(k + 1) * 128])
                else:
                    pe.wait_ge(rope_loaded[2 * b], 16)
                    pe.wait_ge(rope_loaded[2 * b + 1], 16)
                    mm = transpose4(tile_bank[t % 4], lambda k: rope_tok[:, 2 * b + k % 2, (k // 2) * 128:(k // 2 + 1) * 128])
                mm.then_inc(pe_tile, 1)

            def tiles_done(t):
                pe.wait_ge(act_tile, t + 1)
                pe.wait_ge(dve_tile, t + 1)

            def project(kind, half, bank, wready):
                pe.wait_ge(act_whi, wready)
                pe.wait_ge(pool_wlo, wready)
                hi, lo = chunk_dst(kind)
                mh, ml = (cT_hi, cT_lo) if kind < 2 else (xT_hi, xT_lo)
                for k in range(KT):
                    w = slice(k * 128, (k + 1) * 128)
                    tk = slice(half * HT, (half + 1) * HT)
                    mm = three(bank[:, :], (hi[:, w], lo[:, w]), (mh[:, k, tk], ml[:, k, tk]), k == 0, k == KT - 1)
                mm.then_inc(pe_block, 1)

            def bank_free(g, idx):
                p = idx - 2
                u2, j = 2 * g + p // 6, p % 6
                if j == 1:
                    pe.wait_ge(act_v32, u2 + 1)
                else:
                    pe.wait_ge(dve_rot, ropes_until(u2, j))

            def first_block(f):
                if f >= 2:
                    bank_free(0, f)
                project(f % 6, f // 6, f_bank[f % 2], f % 6 + 1)

            pe.wait_ge(ident_done, 1)
            for b in range(4):
                tile("ctx", b)
            tiles_done(tile_of("ctx", 3))
            first_block(0)
            first_block(1)
            tile("rope", 0)
            tile("rope", 1)
            for b in range(4):
                tile("x", b)
            pe.wait_ge(act_v32, 1)
            transpose4(pv_bank, lambda b: v32[:, b * 128:(b + 1) * 128]).then_inc(pe_vT, 1)
            tiles_done(tile_of("x", 3))
            for f in range(2, 6):
                first_block(f)
            for b in range(4, 8):
                tile("ctx", b)
            tiles_done(tile_of("ctx", 7))
            first_block(6)
            for b in range(4, 8):
                tile("x", b)
            tile("rope", 2)
            tile("rope", 3)
            tiles_done(len(TILES) - 1)

            def block_slot(g, c, i):
                idx = AHEAD + 3 * c + i
                if isinstance(g, int) and 12 * g + idx >= BLOCKS:
                    return
                bank_free(g, idx)
                G = g + idx // 12
                project(idx % 6, (idx // 6) % 2, f_bank[idx % 2], W_GROUP * G + idx % 6 + 1)

            def scores(g, c, k):
                n, sl = 8 * g + 2 * c + k, k
                u2, b = 2 * g + c // 2, 2 * (c % 2) + k
                pe.wait_ge(act_qhi, n + 1)
                pe.wait_ge(pool_qlo, n + 1)
                if k == 0:
                    pe.wait_ge(act_khi, u2 + 1)
                    pe.wait_ge(pool_klo, u2 + 1)
                if not (isinstance(n, int) and n < 1):
                    pe.wait_ge(dve_masked, 2 * n)
                ks = (c // 2) % 2
                for h in range(GH):
                    nc.tensor.matmul(s_banks[:, 256 * h:256 * (h + 1)], q_hi[:, sl, h, :], k_parts[:, ks, b, :], start=True, stop=False)
                    mm = nc.tensor.matmul(s_banks[:, 256 * h:256 * h + 128], q_lo[:, sl, h, :], k_parts[:, ks, b, 0:128], start=False, stop=True)
                mm.then_inc(pe_score, 1)

            def prob_transpose(g, c, k):
                n = 8 * g + 2 * c + k
                pe.wait_ge(pool_norm, n + 1)
                pe.wait_ge(act_pThi, n)
                pe.wait_ge(dve_pTlo, n)
                transpose4(t_bank, lambda h: prob[:, k, h, :]).then_inc(pe_pT, 1)

            def pv(g, c, k):
                n = 8 * g + 2 * c + k
                u2, b = 2 * g + c // 2, 2 * (c % 2) + k
                pe.wait_ge(act_pThi, n + 1)
                pe.wait_ge(dve_pTlo, n + 1)
                done = u2 + 1 if last_unit(g, c) else u2 + 2
                pe.wait_ge(act_vhi, done)
                pe.wait_ge(dve_vlo, done)
                pe.wait_ge(act_ohi, n)
                pe.wait_ge(dve_olo, n)
                vs = (c // 2) % 2
                three(pv_bank[:, :], (v_hi[:, vs, b, :], v_lo[:, vs, b, :]),
                      (pT_hi[:, k].rearrange("p h s -> p (h s)"), pT_lo[:, k].rearrange("p h s -> p (h s)")), True, True).then_inc(pe_pv, 1)

            def out_proj(n, k, w_count):
                pe.wait_ge(act_ohi, n + 1)
                pe.wait_ge(dve_olo, n + 1)
                pe.wait_ge(act_whi, w_count)
                pe.wait_ge(pool_wlo, w_count)
                pe.wait_ge(dve_acc, n + 1)
                for h in range(GH):
                    mm = three(o_bank[k][:, :], (o_hi[:, k, h, :], o_lo[:, k, h, :]), (wo_hi[:, h, :], wo_lo[:, h, :]), h == 0, h == GH - 1)
                mm.then_inc(pe_out, 1)

            def pair(g, c):
                first = isinstance(g, int) and 4 * g + c == 0
                u_next = 2 * g + c // 2 + 1
                block_slot(g, c, 0)
                scores(g, c, 1)
                block_slot(g, c, 1)
                wcount = wo_count(g + (c - 1) // 4)
                prob_transpose(g, c, 0)
                if c % 2 == 0:
                    if first:
                        pe.wait_ge(act_vhi, 1)
                        pe.wait_ge(dve_vlo, 1)
                    pe.wait_ge(act_v32, u_next + 1)
                    if not first:
                        pe.wait_ge(act_ohi, 8 * g + 2 * c)
                        pe.wait_ge(dve_olo, 8 * g + 2 * c)
                    transpose4(pv_bank, lambda b: v32[:, b * 128:(b + 1) * 128]).then_inc(pe_vT, 1)
                if not first:
                    out_proj(8 * g + 2 * c - 2, 0, wcount)
                pv(g, c, 0)
                prob_transpose(g, c, 1)
                if not first:
                    out_proj(8 * g + 2 * c - 1, 1, wcount)
                pv(g, c, 1)
                scores(g, c + 1, 0)
                block_slot(g, c, 2)

            def wo_count(G):
                return W_FIRST + W_GROUP * G + GH

            def last_pair(c):
                g, wcount = KVH - 1, wo_count(KVH - 1)
                tiles = iter(range(5 * c - 8, 5 * c - 3))
                out_proj(8 * g + 2 * c - 2, 0, wcount)
                scores(g, c, 1)
                out_proj(8 * g + 2 * c - 1, 1, wcount)
                ffn_tile(next(tiles))
                prob_transpose(g, c, 0)
                ffn_tile(next(tiles))
                ffn_tile(next(tiles))
                pv(g, c, 0)
                prob_transpose(g, c, 1)
                ffn_tile(next(tiles))
                ffn_tile(next(tiles))
                pv(g, c, 1)
                if c == 2:
                    scores(g, 3, 0)

            def ffn_tile(t):
                src, loaded, count = ffn_tile_src(t)
                pe.wait_ge(loaded, count)
                if t < 2:
                    bank_free(KVH - 1, 12 + t)
                else:
                    tiles_done(FFN_T + t - 2)
                transpose4(f_bank[t % 2], lambda k: src[:, k * 128:(k + 1) * 128]).then_inc(pe_tile, 1)

            scores(0, 0, 0)
            pair(0, 0)
            with pe.Fori(0, KVH - 1) as g:
                for c in range(1, 5):
                    pair(g, c)
            pair(KVH - 1, 1)
            ffn_tile(0)
            ffn_tile(1)
            last_pair(2)
            last_pair(3)

            def h_tile(b):
                pe.wait_ge(dve_xn, B + b + 1)
                tiles_done(H_T + b - 2)
                transpose4(f_bank[b % 2], lambda k: xnorm2[:, b % 4, k * 128:(k + 1) * 128]).then_inc(pe_tile, 1)

            def up(half, m):
                i = 4 * half + m
                if i >= 2:
                    pe.wait_ge(dve_gate, i - 1)
                for part in range(2):
                    for k in range(KT):
                        w = slice((4 * part + m) * 128, (4 * part + m + 1) * 128)
                        tk = slice(half * HT, (half + 1) * HT)
                        mm = three(up_bank[2 * (i % 2) + part], (cT_hi[:, k, w], cT_lo[:, k, w]),
                                   (xT_hi[:, k, tk], xT_lo[:, k, tk]), k == 0, k == KT - 1)
                mm.then_inc(pe_up, 1)

            def down(half, b):
                n = 4 * half + b
                a_hi, a_lo = (wo_hi, wo_lo) if half == 0 else (act1_hi, act1_lo)
                if b == 0:
                    pe.wait_ge(act_ghi, 4 * (half + 1))
                    pe.wait_ge(dve_glo, 4 * (half + 1))
                if n == 0:
                    pe.wait_ge(dve_acc, 8 * KVH + 2)
                if n >= 2:
                    pe.wait_ge(dve_out, n - 1)
                for m in range(4):
                    ts = slice(b * 128, (b + 1) * 128)
                    mm = three(o_bank[n % 2][:, :], (a_hi[:, m, ts], a_lo[:, m, ts]), (wq_hi[:, m, :], wq_lo[:, m, :]), m == 0, m == 3)
                mm.then_inc(pe_down, 1)

            n_last = 8 * KVH
            out_proj(n_last - 2, 0, wo_count(KVH - 1))
            out_proj(n_last - 1, 1, wo_count(KVH - 1))
            for b in range(4):
                h_tile(b)
            tiles_done(H_T + 3)
            for m in range(3):
                up(0, m)
            for b in range(4, 8):
                h_tile(b)
            up(0, 3)
            tiles_done(H_T + 7)
            up(1, 0)
            up(1, 1)
            for b in range(4):
                down(0, b)
            up(1, 2)
            up(1, 3)
            for b in range(4):
                down(1, b)

        def k4(bank):
            return bank.rearrange("p (k s) -> p k s", k=4)

        def ffn_tile_dst(t, part):
            if t < 8:
                return (cT_hi, cT_lo)[part][:, :, t * 128:(t + 1) * 128]
            return (wq_hi, wq_lo)[part][:, :, (t - 8) * 128:(t - 7) * 128]

        @block.scalar
        def _(act):
            act.dma_start(pos_raw[:, :], pos.rearrange("b s -> s b"), allow_slow_non_contiguous=True).then_inc(pos_loaded, 16)
            act.dma_start(graw[:, 0:1], g_x.partition_broadcast(128)).then_inc(gate_loaded, 16)
            act.dma_start(graw[:, 1:2], g_f.partition_broadcast(128)).then_inc(gate_loaded, 16)
            act.dma_start(b12_col[:, :], b12.rearrange("(t p) -> p t", p=128), allow_slow_non_contiguous=True).then_inc(bias_loaded, 16)

            def hi(dst, src, s):
                nc.scalar.activation(dst, src, ACT.Copy).then_inc(s, 1)

            act.wait_ge(gate_loaded, 32)
            nc.scalar.activation(small[:, 24:26], graw, ACT.Tanh).then_inc(act_small, 1)

            def tile_copy(what, b):
                t = tile_of(what, b)
                act.wait_ge(pe_tile, t + 1)
                if what == "rope":
                    hi(cosT[:, b * 256:(b + 1) * 256], tile_bank[t % 4][:, 0:256], act_tile)
                else:
                    dst = cT_hi if what == "ctx" else xT_hi
                    hi(dst[:, :, b * 128:(b + 1) * 128], k4(tile_bank[t % 4]), act_tile)

            def split_chunk(done, slot, loaded, dst, free):
                act.wait_ge(raw_loaded[slot], loaded)
                if free is not None:
                    act.wait_ge(*free)
                hi(dst[0], raw[:, slot, :], act_whi)

            def first_chunk(s):
                split_chunk(s + 1, s % RAW, 16 * (s // RAW + 1), chunk_dst(s), None)

            def exps(g, c, k):
                n = 8 * g + 2 * c + k
                act.wait_ge(dve_mask, n + 1)
                for h in range(GH):
                    e = nc.scalar.activation(prob[:, k, h, :], prob[:, k, h, :], ACT.Exp, bias=nmin[k][:, h:h + 1],
                                             scale=-1.0, accum_out=psum_row[k][:, h:h + 1])
                e.then_inc(act_exp, 1)

            def v_copy(g, c):
                u2 = 2 * g + c // 2 + 1
                act.wait_ge(pe_block, 6 * u2 + 2)
                act.wait_ge(pe_vT, u2)
                hi(v32[:, :], f_bank[1][:, :], act_v32)

            def v_hi_copy(u2, vs):
                act.wait_ge(pe_vT, u2 + 1)
                if not (isinstance(u2, int) and u2 < 2):
                    act.wait_ge(pe_pv, 4 * u2 - 4)
                hi(v_hi[:, vs], k4(pv_bank[:, :]), act_vhi)

            def k_hi_copy(u2, ks):
                act.wait_ge(pool_rope, ropes_until(u2, 0))
                if not (isinstance(u2, int) and u2 < 2):
                    act.wait_ge(pe_score, 4 * u2 - 4)
                hi(k_parts[:, ks, :, 0:S], k4(k32[:, :]), act_khi)

            def q_hi_copy(n, u2, qs, k, b):
                act.wait_ge(pool_rope, 5 * u2 + 5)
                if not (isinstance(n, int) and n < 2):
                    act.wait_ge(pe_score, n - 1)
                hi(q_hi[:, k], q32[:, qs, :, b * S:(b + 1) * S], act_qhi)

            def pT_hi_copy(g, c, k):
                n = 8 * g + 2 * c + k
                act.wait_ge(pe_pT, n + 1)
                if not (isinstance(n, int) and n < 2):
                    act.wait_ge(pe_pv, n - 1)
                hi(pT_hi[:, k], k4(t_bank[:, :]), act_pThi)

            def o_hi_copy(g, c, k):
                n = 8 * g + 2 * c + k
                act.wait_ge(pe_pv, n + 1)
                if not (isinstance(n, int) and n < 2):
                    act.wait_ge(pe_out, n - 1)
                hi(o_hi[:, k], k4(pv_bank[:, :]), act_ohi)

            for b in range(4):
                tile_copy("ctx", b)
            first_chunk(0)
            first_chunk(1)
            act.wait_ge(pe_block, 2)
            hi(v32[:, :], f_bank[1][:, :], act_v32)
            tile_copy("rope", 0)
            tile_copy("rope", 1)
            first_chunk(2)
            for b in range(4):
                tile_copy("x", b)
            v_hi_copy(0, 0)
            for s in range(3, 6):
                first_chunk(s)
            k_hi_copy(0, 0)
            for b in range(4, 8):
                tile_copy("ctx", b)
            for b in range(4, 8):
                tile_copy("x", b)
            tile_copy("rope", 2)
            tile_copy("rope", 3)
            q_hi_copy(0, 0, 0, 0, 0)
            q_hi_copy(1, 0, 0, 1, 1)

            def ffn_tile_copy(t):
                act.wait_ge(pe_tile, FFN_T + t + 1)
                hi(ffn_tile_dst(t, 0), k4(f_bank[t % 2][:, :]), act_tile)

            def pair(g, c):
                u2 = 2 * g + c // 2
                chunks = pair_chunks(g, c)
                exps(g, c, 0)
                if c % 4:
                    for ch in chunks[:1]:
                        split_chunk(*ch)
                if c % 2 == 0:
                    v_copy(g, c)
                    k_hi_copy(u2 + 1, (c // 2 + 1) % 2)
                elif c % 4:
                    for ch in chunks[1:2]:
                        split_chunk(*ch)
                exps(g, c, 1)
                pT_hi_copy(g, c, 0)
                if c % 2 == 0:
                    v_hi_copy(u2 + 1, (c // 2 + 1) % 2)
                if c % 4:
                    for ch in chunks[2 if c % 2 else 1:]:
                        split_chunk(*ch)
                o_hi_copy(g, c, 0)
                pT_hi_copy(g, c, 1)
                next_queries(g, c)
                o_hi_copy(g, c, 1)
                if c % 4 == 0:
                    for ch in chunks:
                        split_chunk(*ch)

            def next_queries(g, c):
                for k in range(2):
                    q_hi_copy(8 * g + 2 * c + 2 + k, 2 * g + (c + 1) // 2, ((c + 1) // 2) % 2, k, 2 * ((c + 1) % 2) + k)

            def last_pair(c):
                g = KVH - 1
                tiles = iter(range(5 * c - 8, 5 * c - 3))
                exps(g, c, 0)
                exps(g, c, 1)
                if c == 2:
                    next_queries(g, c)
                ffn_tile_copy(next(tiles))
                pT_hi_copy(g, c, 0)
                ffn_tile_copy(next(tiles))
                ffn_tile_copy(next(tiles))
                o_hi_copy(g, c, 0)
                pT_hi_copy(g, c, 1)
                ffn_tile_copy(next(tiles))
                ffn_tile_copy(next(tiles))
                o_hi_copy(g, c, 1)

            pair(0, 0)
            with act.Fori(0, KVH - 1) as g:
                for c in range(1, 5):
                    pair(g, c)
            pair(KVH - 1, 1)
            ffn_tile_copy(0)
            ffn_tile_copy(1)
            last_pair(2)
            last_pair(3)

            def h_copy(b):
                act.wait_ge(pe_tile, H_T + b + 1)
                hi(xT_hi[:, :, b * 128:(b + 1) * 128], k4(f_bank[b % 2][:, :]), act_tile)

            def gate(half, m):
                i = 4 * half + m
                a_hi = wo_hi if half == 0 else act1_hi
                act.wait_ge(pe_up, i + 1)
                if i >= 2:
                    act.wait_ge(dve_gate, i - 1)
                nc.scalar.activation(t_cos[:, i % 2, :], up_bank[2 * (i % 2)], ACT.Silu, bias=b12_col[:, m:m + 1]).then_inc(act_silu, 1)
                act.wait_ge(dve_gate, i + 1)
                if i == 0:
                    act.wait_ge(pe_out, 8 * KVH)
                hi(a_hi[:, m, :], t_sin[:, i % 2, :], act_ghi)

            for b in range(4):
                h_copy(b)
            act.wait_ge(bias_loaded, 16)
            for m in range(3):
                gate(0, m)
            for b in range(4, 8):
                h_copy(b)
            gate(0, 3)
            for m in range(4):
                gate(1, m)

        @block.gpsimd
        def _(pool):
            pool.memset(ident[:, :], 0.0).then_inc(ident_zero, 1)
            pool.wait_ge(ident_zero, 1)
            pool.affine_select(out=ident[:, :], in_=ident[:, :], compare_op=ALU.not_equal, fill=1.0, base=0,
                               pattern=[[-1, 128]], channel_multiplier=1).then_inc(ident_done, 1)
            pool.wait_ge(dve_small, 3)

            def gather(b):
                pool.indirect_dma_start(rope_tok[:, b, :], None, table[:, :],
                                        bass.IndirectOffsetOnAxis(ap=pos_fix[:, b:b + 1], axis=0)).then_inc(rope_loaded[b], 16)

            def minus(dst, a, b_, s):
                nc.gpsimd.tensor_tensor(dst, a, b_, ALU.subtract).then_inc(s, 1)

            def split_chunk(done, slot, loaded, dst, free):
                pool.wait_ge(act_whi, done)
                minus(dst[1], raw[:, slot, :], f32(dst[0]), pool_wlo)


            def rope_add(g, idx):
                u2, j = 2 * g + idx // 6, idx % 6
                cnt = ropes_until(u2, j)
                ts = rope_slot(idx)
                pool.wait_ge(dve_rot, cnt)
                fixed = isinstance(g, int)
                if j == 0:
                    if not (fixed and 12 * g + idx < 6):
                        pool.wait_ge(act_khi, u2)
                        pool.wait_ge(pool_klo, u2)
                    dst = k32[:, :]
                else:
                    if not (fixed and 12 * g + idx < 12):
                        pool.wait_ge(act_qhi, 4 * u2 - 4)
                        pool.wait_ge(pool_qlo, 4 * u2 - 4)
                    dst = q32[:, (idx // 6) % 2, j - 2, :]
                nc.gpsimd.tensor_tensor(dst, t_cos[:, ts, :], t_sin[:, ts, :], ALU.add).then_inc(pool_rope, 1)

            def k_lo_split(u2, ks):
                pool.wait_ge(act_khi, u2 + 1)
                minus(k_parts[:, ks, :, S:2 * S], k4(k32[:, :]), f32(k_parts[:, ks, :, 0:S]), pool_klo)

            def q_lo_split(n, qs, k, b):
                pool.wait_ge(act_qhi, n + 1)
                minus(q_lo[:, k], q32[:, qs, :, b * S:(b + 1) * S], f32(q_hi[:, k]), pool_qlo)

            def norm(g, c, k):
                n = 8 * g + 2 * c + k
                pool.wait_ge(dve_recip, n + 1)
                nc.gpsimd.tensor_tensor(prob[:, k], prob[:, k], rrow[k].unsqueeze(2).to_broadcast([128, GH, S]), ALU.mult).then_inc(pool_norm, 1)

            def first_chunk(s):
                split_chunk(s + 1, s % RAW, None, chunk_dst(s), None)

            for b in range(4):
                gather(b)
            first_chunk(0)
            first_chunk(1)
            for b in range(4, 8):
                gather(b)
            first_chunk(2)
            rope_add(0, 0)
            for s in range(3, 6):
                first_chunk(s)
            k_lo_split(0, 0)
            for f in range(2, 6):
                rope_add(0, f)
            q_lo_split(0, 0, 0, 0)
            q_lo_split(1, 0, 1, 1)

            def pair(g, c):
                u2 = 2 * g + c // 2
                idx = AHEAD + 3 * c
                chunks = pair_chunks(g, c)
                rope_add(g, idx - 1)
                norm(g, c, 0)
                if c % 2 == 0:
                    k_lo_split(u2 + 1, (c // 2 + 1) % 2)
                early = 2 if c % 2 else 1
                if c % 4:
                    for ch in chunks[:early]:
                        split_chunk(*ch)
                norm(g, c, 1)
                if c % 4:
                    for ch in chunks[early:]:
                        split_chunk(*ch)
                if c % 2:
                    rope_add(g, idx)
                    rope_add(g, idx + 1)
                    next_queries(g, c)
                else:
                    next_queries(g, c)
                    rope_add(g, idx + 1)
                if c % 4 == 0:
                    for ch in chunks:
                        split_chunk(*ch)

            def next_queries(g, c):
                for k in range(2):
                    q_lo_split(8 * g + 2 * c + 2 + k, ((c + 1) // 2) % 2, k, 2 * ((c + 1) % 2) + k)

            pair(0, 0)
            with pool.Fori(0, KVH - 1) as g:
                for c in range(1, 5):
                    pair(g, c)
            pair(KVH - 1, 1)
            norm(KVH - 1, 2, 0)
            norm(KVH - 1, 2, 1)
            next_queries(KVH - 1, 2)
            norm(KVH - 1, 3, 0)
            norm(KVH - 1, 3, 1)

        @block.vector
        def _(dve):
            dve.sem_inc(dve_acc, 2)
            dve.wait_ge(pos_loaded, 16)
            nc.vector.tensor_scalar(posf, pos_raw[:, :], 0.0, float(MAX_POS), ALU.is_lt, ALU.mult).then_inc(dve_small, 1)
            dve.wait_ge(dve_small, 1)
            nc.vector.tensor_tensor(posf, posf, pos_raw[:, :], ALU.add).then_inc(dve_small, 1)
            dve.wait_ge(dve_small, 2)
            nc.vector.tensor_scalar(pos_fix[:, :], posf, 0.0, float(MAX_POS - 1), ALU.max, ALU.min).then_inc(dve_small, 1)

            def lo(dst, src, hi_part, s):
                nc.vector.tensor_tensor(dst, src, f32(hi_part), ALU.subtract).then_inc(s, 1)

            def stats_of(b, s_cnt):
                nc.vector.bn_stats(stats, resid[:, b, :]).then_inc(dve_st, 1)
                dve.wait_ge(dve_st, s_cnt + 1)
                nc.vector.bn_aggr(mv[:, b, :], stats).then_inc(dve_st, 1)
                dve.wait_ge(dve_st, s_cnt + 2)

            def inv_std(b0, b1, done):
                v, y, t = var[:, b0:b1], rstd[:, b0:b1], newton[:, b0:b1]

                def after(op):
                    nonlocal done
                    op.then_inc(dve_newton, 1)
                    done += 1
                    dve.wait_ge(dve_newton, done)
                after(nc.vector.tensor_scalar(v, mv[:, b0:b1, 1], EPS, None, ALU.add))
                after(nc.vector.tensor_scalar(y.bitcast(I32), v.bitcast(I32), -0.5, float(0x5F3759DF), ALU.mult, ALU.add))
                for _ in range(NEWTON):
                    after(nc.vector.scalar_tensor_tensor(out=t, in0=y, scalar=-0.5, in1=y, op0=ALU.mult, op1=ALU.mult))
                    after(nc.vector.tensor_tensor(t, t, v, ALU.mult))
                    after(nc.vector.scalar_tensor_tensor(out=y, in0=t, scalar=1.5, in1=y, op0=ALU.add, op1=ALU.mult))

            def tile_lo(what, b):
                t = tile_of(what, b)
                bank = tile_bank[t % 4]
                dve.wait_ge(act_tile, t + 1)
                if what == "rope":
                    nc.vector.tensor_copy(sinT[:, b * 256:(b + 1) * 256], bank[:, 256:512]).then_inc(dve_tile, 1)
                else:
                    dst, h = (cT_lo, cT_hi) if what == "ctx" else (xT_lo, xT_hi)
                    sl = slice(b * 128, (b + 1) * 128)
                    lo(dst[:, :, sl], k4(bank), h[:, :, sl], dve_tile)

            def normalise(dst, b):
                nc.vector.tensor_scalar(dst, resid[:, b, :], mv[:, b, 0:1], rstd[:, b:b + 1], ALU.subtract, ALU.mult).then_inc(dve_xn, 1)

            def x_stats(b):
                dve.wait_ge(x_loaded[b], 16)
                stats_of(b, 2 * b)

            def x_norm(b):
                if b >= 2:
                    dve.wait_ge(pe_tile, tile_of("x", b - 2) + 1)
                normalise(xnorm[:, b % 2, :], b)

            def rotate(g, idx):
                u2, j, half = 2 * g + idx // 6, idx % 6, (idx // 6) % 2
                fixed = isinstance(g, int)
                bank = f_bank[idx % 2]
                ts = rope_slot(idx)
                f_cnt = 12 * g + idx + 1
                dve.wait_ge(pe_block, f_cnt)
                cnt = ropes_until(u2, j)
                if not (fixed and ropes_until(2 * g + idx // 6, j) <= 2):
                    dve.wait_ge(pool_rope, cnt - 2)
                if fixed and 12 * g + idx in (0, 6):
                    dve.wait_ge(act_tile, tile_of("rope", 2 * half + 1) + 1)
                    dve.wait_ge(dve_tile, tile_of("rope", 2 * half + 1) + 1)
                tk = slice(half * HT, (half + 1) * HT)

                def times(dst, a, b_):
                    if j == 0:
                        return nc.vector.scalar_tensor_tensor(out=dst, in0=a, scalar=SCORE_SCALE, in1=b_, op0=ALU.mult, op1=ALU.mult)
                    return nc.vector.tensor_tensor(dst, a, b_, ALU.mult)
                times(t_cos[:, ts, :], bank[:, :], cosT[:, tk])
                times(t_sin[64:128, ts, :], bank[0:64, :], sinT[0:64, tk])
                times(t_sin[0:64, ts, :], bank[64:128, :], sinT[64:128, tk]).then_inc(dve_rot, 1)

            def v_lo_split(u2, vs):
                dve.wait_ge(act_vhi, u2 + 1)
                lo(v_lo[:, vs], k4(pv_bank[:, :]), v_hi[:, vs], dve_vlo)

            for b in range(4):
                tile_lo("ctx", b)
            for b in range(4):
                x_stats(b)
            inv_std(0, 4, 0)
            x_norm(0)
            x_norm(1)
            tile_lo("rope", 0)
            tile_lo("rope", 1)
            for b in range(4):
                tile_lo("x", b)
                if b < 2:
                    x_norm(b + 2)
            rotate(0, 0)
            v_lo_split(0, 0)
            for b in range(4):
                rotate(0, b + 2)
                x_stats(b + 4)
            inv_std(4, 8, NEWTON_OPS)
            x_norm(4)
            x_norm(5)
            for b in range(4, 8):
                tile_lo("ctx", b)
            for b in range(4, 8):
                tile_lo("x", b)
                if b < 6:
                    x_norm(b + 2)
            tile_lo("rope", 2)
            tile_lo("rope", 3)
            dve.wait_ge(mask_loaded, 16)
            nc.vector.tensor_scalar(mfill[:, :, :], mask_raw[:, :, :], 0.0, MASKED, ALU.is_equal, ALU.mult).then_inc(dve_small, 1)

            def mask_scores(g, c, k):
                n = 8 * g + 2 * c + k
                dve.wait_ge(pe_score, n + 1)
                if not (isinstance(n, int) and n < 2):
                    dve.wait_ge(pe_pT, n - 1)
                b = (2 * c + k) % B
                if first_step(n):
                    dve.wait_ge(dve_small, 4)
                nc.vector.tensor_tensor(prob[:, k], s_parts[:, :, 1, :], mfill[:, b, :].unsqueeze(1).to_broadcast([128, GH, S]),
                                        ALU.add).then_inc(dve_masked, 1)
                dve.wait_ge(dve_masked, 2 * n + 1)
                nc.vector.tensor_tensor(prob[:, k], s_parts[:, :, 0, :], prob[:, k], ALU.add).then_inc(dve_masked, 1)
                dve.wait_ge(dve_masked, 2 * n + 2)
                nc.vector.tensor_reduce(nmin[k], prob[:, k], mybir.AxisListType.X, ALU.min).then_inc(dve_mask, 1)

            def first_step(n):
                return isinstance(n, int) and n == 0

            def recip(g, c, k):
                dve.wait_ge(act_exp, 8 * g + 2 * c + k + 1)
                nc.vector.reciprocal(rrow[k], psum_row[k]).then_inc(dve_recip, 1)

            def pT_lo_split(g, c, k):
                dve.wait_ge(act_pThi, 8 * g + 2 * c + k + 1)
                lo(pT_lo[:, k], k4(t_bank[:, :]), pT_hi[:, k], dve_pTlo)

            def o_lo_split(g, c, k):
                dve.wait_ge(act_ohi, 8 * g + 2 * c + k + 1)
                lo(o_lo[:, k], k4(pv_bank[:, :]), o_hi[:, k], dve_olo)

            def add_out(n, b, k):
                dve.wait_ge(pe_out, n + 1)
                nc.vector.scalar_tensor_tensor(out=resid[:, b, :], in0=o_bank[k][:, :], scalar=tg_x, in1=resid[:, b, :],
                                               op0=ALU.mult, op1=ALU.add).then_inc(dve_acc, 1)

            def ffn_tile_lo(t):
                dve.wait_ge(act_tile, FFN_T + t + 1)
                lo(ffn_tile_dst(t, 1), k4(f_bank[t % 2][:, :]), ffn_tile_dst(t, 0), dve_tile)

            def pair(g, c):
                u2 = 2 * g + c // 2
                idx = AHEAD + 3 * c
                fixed = isinstance(g, int)
                rotate(g, idx - 1)
                recip(g, c, 0)
                mask_scores(g, c, 1)
                if c % 2:
                    rotate(g, idx)
                recip(g, c, 1)
                pT_lo_split(g, c, 0)
                if c % 2 == 0:
                    v_lo_split(u2 + 1, (c // 2 + 1) % 2)
                rotate(g, idx + 1)
                first = fixed and 4 * g + c == 0
                if not first:
                    add_out(8 * g + 2 * c - 2, (2 * c - 2) % B, 0)
                o_lo_split(g, c, 0)
                pT_lo_split(g, c, 1)
                if not first:
                    add_out(8 * g + 2 * c - 1, (2 * c - 1) % B, 1)
                o_lo_split(g, c, 1)
                mask_scores(g, c + 1, 0)

            def last_pair(c):
                g = KVH - 1
                tiles = iter(range(5 * c - 8, 5 * c - 3))
                recip(g, c, 0)
                add_out(8 * g + 2 * c - 2, (2 * c - 2) % B, 0)
                mask_scores(g, c, 1)
                recip(g, c, 1)
                add_out(8 * g + 2 * c - 1, (2 * c - 1) % B, 1)
                ffn_tile_lo(next(tiles))
                pT_lo_split(g, c, 0)
                ffn_tile_lo(next(tiles))
                ffn_tile_lo(next(tiles))
                o_lo_split(g, c, 0)
                pT_lo_split(g, c, 1)
                ffn_tile_lo(next(tiles))
                ffn_tile_lo(next(tiles))
                o_lo_split(g, c, 1)
                if c == 2:
                    mask_scores(g, 3, 0)

            def h_stats(b):
                dve.wait_ge(dve_acc, 2 + 8 * (KVH - 1) + b + 1)
                stats_of(b, 2 * B + 2 * b)

            def h_norm(b):
                if b >= 4:
                    dve.wait_ge(pe_tile, H_T + b - 4 + 1)
                normalise(xnorm2[:, b % 4, :], b)

            def h_lo(b):
                dve.wait_ge(act_tile, H_T + b + 1)
                sl = slice(b * 128, (b + 1) * 128)
                lo(xT_lo[:, :, sl], k4(f_bank[b % 2][:, :]), xT_hi[:, :, sl], dve_tile)

            dve.wait_ge(act_small, 1)
            mask_scores(0, 0, 0)
            pair(0, 0)
            with dve.Fori(0, KVH - 1) as g:
                for c in range(1, 5):
                    pair(g, c)
            pair(KVH - 1, 1)
            ffn_tile_lo(0)
            ffn_tile_lo(1)
            last_pair(2)
            for b in range(4):
                h_stats(b)
            last_pair(3)

            inv_std(0, 4, 2 * NEWTON_OPS)
            for b in range(4):
                h_norm(b)
            h_stats(4)
            h_stats(5)
            add_out(8 * KVH - 2, 6, 0)
            add_out(8 * KVH - 1, 7, 1)
            for b in range(4):
                h_lo(b)
            h_stats(6)
            h_stats(7)
            inv_std(4, 8, 3 * NEWTON_OPS)
            for b in range(4, 8):
                h_norm(b)
            dve.wait_ge(bias3_loaded, 16)

            def gate(half, m):
                i = 4 * half + m
                a_hi, a_lo = (wo_hi, wo_lo) if half == 0 else (act1_hi, act1_lo)
                dve.wait_ge(act_silu, i + 1)
                if i >= 2:
                    dve.wait_ge(act_ghi, i - 1)
                    dve.wait_ge(dve_glo, i - 1)
                nc.vector.scalar_tensor_tensor(out=t_sin[:, i % 2, :], in0=up_bank[2 * (i % 2) + 1], scalar=b12_col[:, 4 + m:5 + m],
                                               in1=t_cos[:, i % 2, :], op0=ALU.add, op1=ALU.mult).then_inc(dve_gate, 1)
                dve.wait_ge(act_ghi, i + 1)
                lo(a_lo[:, m, :], t_sin[:, i % 2, :], a_hi[:, m, :], dve_glo)
                nc.vector.scalar_tensor_tensor(out=resid[:, i, :], in0=b3_row[:, :], scalar=tg_f, in1=resid[:, i, :],
                                               op0=ALU.mult, op1=ALU.add).then_inc(dve_b3, 1)

            def result(n):
                dve.wait_ge(pe_down, n + 1)
                dve.wait_ge(dve_b3, n + 1)
                nc.vector.scalar_tensor_tensor(out=resid[:, n, :], in0=o_bank[n % 2][:, :], scalar=tg_f, in1=resid[:, n, :],
                                               op0=ALU.mult, op1=ALU.add).then_inc(dve_out, 1)

            for m in range(3):
                gate(0, m)
            for b in range(4, 8):
                h_lo(b)
            gate(0, 3)
            gate(1, 0)
            gate(1, 1)
            for n in range(4):
                result(n)
            gate(1, 2)
            gate(1, 3)
            for n in range(4, 8):
                result(n)


_INS = ['x', 'ctx_4096', 'pos_BxS2', 'mask_BxSxS2_ik0', 'g_xattn', 'g_ffn', 'L0_xattn_Wq', 'L0_xattn_Wk', 'L0_xattn_Wv',
        'L0_xattn_Wo', 'L0_ffn_w12', 'L0_ffn_b12', 'L0_ffn_w3', 'L0_ffn_b3']
_OUTS = [((8, 128, 512), 'float32')]


def kernel(**inputs):
    import numpy as _np
    import concourse.bacc as _bacc
    from concourse import mybir as _mybir
    from concourse.bass_utils import run_bass_kernel_spmd as _run

    nc = _bacc.Bacc("TRN2", target_bir_lowering=False, num_devices=1, dynamic_dma_scratch_size=4096)
    arrays, args = {}, []
    for name in _INS:
        a = _np.ascontiguousarray(inputs[name])
        arrays[f"in_{name}_dram"] = a
        args.append(nc.dram_tensor(f"in_{name}_dram", a.shape, _mybir.dt.from_np(a.dtype), kind="ExternalInput").ap())
    for i, (shape, dtype) in enumerate(_OUTS):
        dt = _mybir.dt.from_np(_np.dtype(dtype))
        args.append(nc.dram_tensor(f"out_{i}_dram", shape, dt, kind="ExternalOutput").ap())
    build(nc, *args)
    r = _run(nc, [arrays], core_ids=[0])
    return r.results[0]["out_0_dram"]
```

```python
import concourse.bass as bass
import numpy as np
from concourse import mybir
from contextlib import ExitStack

F32 = mybir.dt.float32
F32R = mybir.dt.float32r
I32 = mybir.dt.int32
ALU = mybir.AluOpType
ACT = mybir.ActivationFunctionType

B, S, E = 8, 128, 512
H, KVH, D = 32, 8, 128
GH = H // KVH
KT = E // 128
TOK = B * S
HB = B // 2
HT = HB * S
M = 512
MAX_POS, THETA = 512, 10000.0
EPS = 1e-5
SCORE_SCALE = -1.0 / float(np.sqrt(np.float32(D)))
MASKED = float(2.0 ** 100)

NEWTON = 3
NEWTON_OPS = 2 + 3 * NEWTON

UNITS = 2 * KVH
BLOCKS = 6 * UNITS
AHEAD = 7
PAIRS = 2 * UNITS
RAW = 5
W_FIRST, W_GROUP = 6, 10


def rope_table():
    inv_freq = (1.0 / THETA ** (np.arange(0, D, 2, dtype=np.float32) / np.float32(D))).astype(np.float32)
    angle = np.arange(MAX_POS, dtype=np.float32)[:, None] * inv_freq[None, :]
    c, s = np.cos(angle), np.sin(angle)
    return np.ascontiguousarray(np.concatenate([c, c, s, -s], axis=1).astype(np.float32))


def block_of(f):
    return f % 6


def ropes_until(u2, j):
    return 5 * u2 + (1 if j == 0 else j)


def build(nc, x, ctx, pos, mask, g_x, g_f, Wq, Wk, Wv, Wo, w12, b12, w3, b3, out):
    table = nc.inline_tensor(rope_table(), "rope_table")
    table = table.ap() if hasattr(table, "ap") else table
    es = ExitStack()
    base = (nc.sbuf_base + 31) // 32 * 32
    at = {"top": base}

    def place(name, shape, dt, offset=None):
        size = int(np.prod(shape[1:])) * 4
        if offset is None:
            offset = at["top"]
            at["top"] += (size + 31) // 32 * 32
        at[name] = offset
        return nc.alloc_sbuf_tensor_at(name, shape, dt, offset=offset)

    def sem(name):
        return es.enter_context(nc.semaphore(name))

    with es:
        xT_hi, xT_lo = place("xT_hi", [128, KT, TOK], F32R), place("xT_lo", [128, KT, TOK], F32R)
        cT_hi, cT_lo = place("cT_hi", [128, KT, TOK], F32R), place("cT_lo", [128, KT, TOK], F32R)
        resid = place("resid", [128, B, E], F32)
        wq_hi, wq_lo = place("wq_hi", [128, GH, KT * 128], F32R), place("wq_lo", [128, GH, KT * 128], F32R)
        wk_hi, wk_lo = place("wk_hi", [128, KT * 128], F32R), place("wk_lo", [128, KT * 128], F32R)
        wv_hi, wv_lo = place("wv_hi", [128, KT * 128], F32R), place("wv_lo", [128, KT * 128], F32R)
        wo_hi, wo_lo = place("wo_hi", [128, GH, E], F32R), place("wo_lo", [128, GH, E], F32R)
        raw = place("raw", [128, RAW, 512], F32)
        cosT, sinT = place("cosT", [128, TOK], F32), place("sinT", [128, TOK], F32)
        mfill = place("mfill", [128, B, S], F32)
        q32 = place("q32", [128, 2, GH, HT], F32)
        q_hi, q_lo = place("q_hi", [128, 2, GH, S], F32R), place("q_lo", [128, 2, GH, S], F32R)
        k_parts = place("k_parts", [128, 2, HB, 2 * S], F32R)
        v_hi, v_lo = place("v_hi", [128, 2, HB, D], F32R), place("v_lo", [128, 2, HB, D], F32R)
        k32, v32 = place("k32", [128, HT], F32), place("v32", [128, HT], F32)
        t_cos, t_sin = place("t_cos", [128, 2, HT], F32), place("t_sin", [128, 2, HT], F32)
        prob = place("prob", [128, 2, GH, S], F32)
        pT_hi, pT_lo = place("pT_hi", [128, 2, GH, S], F32R), place("pT_lo", [128, 2, GH, S], F32R)
        o_hi, o_lo = place("o_hi", [128, 2, GH, S], F32R), place("o_lo", [128, 2, GH, S], F32R)
        xnorm = place("xnorm", [128, B, E], F32, at["wo_hi"])
        ident = place("ident", [128, 128], F32)
        small = place("small", [128, 128], F32)
        ctx_raw = place("ctx_raw", [128, B, E], F32, at["q32"])
        rope_tok = place("rope_tok", [128, B, 256], F32, at["pT_hi"])
        mask_raw = place("mask_raw", [128, B, S], I32, at["o_hi"])
        ffn_raw = place("ffn_raw", [128, 4, 512], F32, at["wk_hi"])
        ffn_raw2 = place("ffn_raw2", [128, 4, 512], F32, at["q32"])
        xnorm2 = place("xnorm2", [128, 4, E], F32, at["cosT"])
        act1_hi = place("act1_hi", [128, 4, HT], F32R, at["q32"])
        act1_lo = place("act1_lo", [128, 4, HT], F32R, at["q32"] + 4 * HT * 4)
        b3_row = place("b3_row", [128, E], F32, at["k32"])
        pos_raw = place("pos_raw", [128, B], I32)
        pos_fix = place("pos_fix", [128, B], I32)
        b12_col = place("b12_col", [128, 8], F32)

        def col(i, n=1):
            return small[:, i:i + n]
        nmin = [small[:, 0:4], small[:, 4:8]]
        psum_row = [small[:, 8:12], small[:, 12:16]]
        rrow = [small[:, 16:20], small[:, 20:24]]
        tg_x, tg_f = col(24), col(25)
        graw = col(26, 2)
        mv = small[:, 32:48].rearrange("p (b t) -> p b t", t=2)
        var = col(48, 8)
        rstd = col(56, 8)
        newton = col(80, 8)
        posf = col(64, 8)
        stats = small[:, 72:78]
        shift = col(88, 8)

        def bank(name, n=1):
            return es.enter_context(nc.psum_tensor(name, [128, 512 * n], F32))
        f_bank = [bank("f_bank0"), bank("f_bank1")]
        s_banks, t_bank, pv_bank = bank("s_banks", 2), bank("t_bank"), bank("pv_bank")
        o_bank = [bank("o_bank0"), bank("o_bank1")]
        s_parts = s_banks[:, :].rearrange("p (h two k) -> p h two k", h=GH, two=2)
        up_bank = [s_banks[:, 0:512], s_banks[:, 512:1024], t_bank[:, :], pv_bank[:, :]]

        x_loaded = [sem(f"x_loaded{i}") for i in range(B)]
        ctx_loaded = [sem(f"ctx_loaded{i}") for i in range(B)]
        pos_loaded, mask_loaded, gate_loaded, bias_loaded = sem("pos_loaded"), sem("mask_loaded"), sem("gate_loaded"), sem("bias_loaded")
        rope_loaded = [sem(f"rope_loaded{i}") for i in range(B)]
        raw_loaded = [sem(f"raw_loaded{i}") for i in range(RAW)]
        ffn_loaded = [sem(f"ffn_loaded{i}") for i in range(7)]
        out_stored = sem("out_stored")
        ident_zero, ident_done = sem("ident_zero"), sem("ident_done")
        dve_small, act_small = sem("dve_small"), sem("act_small")
        pe_tile, act_tile, dve_tile = sem("pe_tile"), sem("act_tile"), sem("dve_tile")
        pe_block, pe_vT, pe_score, pe_pT, pe_pv, pe_out = (sem(n) for n in ("pe_block", "pe_vT", "pe_score", "pe_pT", "pe_pv", "pe_out"))
        dve_rot, pool_rope, act_khi, pool_klo = (sem(n) for n in ("dve_rot", "pool_rope", "act_khi", "pool_klo"))
        act_v32, act_vhi, dve_vlo = (sem(n) for n in ("act_v32", "act_vhi", "dve_vlo"))
        act_qhi, dve_qlo, pool_qlo = sem("act_qhi"), sem("dve_qlo"), sem("pool_qlo")
        dve_mask, act_exp, dve_recip, pool_norm = (sem(n) for n in ("dve_mask", "act_exp", "dve_recip", "pool_norm"))
        act_pThi, dve_pTlo, act_ohi, dve_olo, dve_acc = (sem(n) for n in ("act_pThi", "dve_pTlo", "act_ohi", "dve_olo", "dve_acc"))
        act_whi, pool_wlo = sem("act_whi"), sem("pool_wlo")
        pe_up, act_silu, dve_gate, act_ghi, dve_glo, pe_down, dve_out, dve_st, dve_b3, bias3_loaded, dve_masked = (sem(n) for n in (
            "pe_up", "act_silu", "dve_gate", "act_ghi", "dve_glo", "pe_down", "dve_out", "dve_st", "dve_b3", "bias3_loaded", "dve_masked"))
        dve_newton, act_xn = sem("dve_newton"), sem("act_xn")
        pe_ftile, act_fstage, act_fhi, pool_flo = (sem(n) for n in ("pe_ftile", "act_fstage", "act_fhi", "pool_flo"))
        dve_shift = sem("dve_shift")
        block = es.enter_context(nc.Block())

        def f32(ap):
            return ap.bitcast(F32)

        def last_unit(g, c):
            return isinstance(g, int) and 2 * g + c // 2 == UNITS - 1

        def chunk_src(kind, group):
            if kind == 0 or kind == 1:
                w = Wk if kind == 0 else Wv
                return w[:, bass.ds(group * D, D)].rearrange("(t p) c -> p t c", p=128)
            return Wq[:, bass.ds(group * (GH * D) + (kind - 2) * D, D)].rearrange("(t p) c -> p t c", p=128)

        def wo_src(group, h):
            return Wo[bass.ds(group * (GH * D) + h * D, D), :]

        def chunk_dst(kind):
            if kind == 0:
                return wk_hi[:, :], wk_lo[:, :]
            if kind == 1:
                return wv_hi[:, :], wv_lo[:, :]
            return wq_hi[:, kind - 2, :], wq_lo[:, kind - 2, :]

        def pair_chunks(g, c):
            r, G = c % 4, g + c // 4

            def chunk(off, dst, free):
                return W_GROUP * G + off + 1, off % RAW, 16 * (W_GROUP // RAW * G + off // RAW + 1), dst, free
            if r == 0:
                first = isinstance(G, int) and G == 0
                return [chunk(W_FIRST + h, (wo_hi[:, h, :], wo_lo[:, h, :]), None if first else (pe_out, 8 * G)) for h in range(GH)]
            if isinstance(G, int) and G == KVH - 1:
                return []
            return [chunk(W_GROUP + kind, chunk_dst(kind), (pe_block, 12 * G + 6 + kind + 1)) for kind in {1: [0, 1, 2], 2: [3, 4, 5], 3: []}[r]]

        def rope_slot(idx):
            return (ropes_until(idx // 6, idx % 6) - 1) % 2

        TILES = [("ctx", b) for b in range(4)] + [("rope", 0), ("rope", 1)] + [("x", b) for b in range(4)] + \
                [("ctx", b) for b in range(4, 8)] + [("rope", 2), ("rope", 3)] + [("x", b) for b in range(4, 8)]
        H_T = len(TILES)
        FFN_TILES = 12

        def tile_of(what, b):
            return TILES.index((what, b))

        def tile_bank(t):
            if t >= len(TILES) - 4:
                return o_bank[t % 2][:, :]
            return (s_banks[:, 0:512], s_banks[:, 512:1024], o_bank[0][:, :], o_bank[1][:, :])[t % 4]

        def h_bank(b):
            return (f_bank[0], f_bank[1], t_bank, pv_bank, *f_bank, *f_bank)[b]

        def ffn_tile_src(t):
            if t < RAW:
                return raw[:, t, :], raw_loaded[t], 16 * ((W_FIRST + W_GROUP * KVH - 6 + t) // RAW + 1)
            if t < RAW + 4:
                return ffn_raw[:, t - RAW, :], ffn_loaded[t - RAW], 16
            return ffn_raw2[:, t - RAW - 4, :], ffn_loaded[t - RAW], 16

        @block.sync
        def _(sp):
            def rows(dst, src, b, s):
                sp.dma_start(dst[:, b, :], src[b]).then_inc(s[b], 16)

            def first_chunk(s):
                sp.dma_start(raw[:, s, :].rearrange("p (t c) -> p t c", t=KT), chunk_src(s, 0)).then_inc(raw_loaded[s], 16)
            for b in range(2):
                rows(ctx_raw, ctx, b, ctx_loaded)
            first_chunk(0)
            for b in range(2, 4):
                rows(ctx_raw, ctx, b, ctx_loaded)
            first_chunk(1)
            for b in range(4):
                rows(resid, x, b, x_loaded)
            for s in range(2, RAW):
                first_chunk(s)
            for b in range(4, 8):
                rows(ctx_raw, ctx, b, ctx_loaded)
            for b in range(4, 8):
                rows(resid, x, b, x_loaded)
            sp.dma_start(mask_raw[:, :, :], mask.rearrange("b q k -> q b k")).then_inc(mask_loaded, 16)

            def load_chunk(s, slot, src, parts):
                sp.wait_ge(act_whi, s - RAW + 1)
                sp.wait_ge(pool_wlo, s - RAW + 1)
                dst = raw[:, slot, :]
                if parts:
                    dst = dst.rearrange("p (t c) -> p t c", t=KT)
                sp.dma_start(dst, src).then_inc(raw_loaded[slot], 16)

            load_chunk(5, 0, chunk_src(5, 0), True)

            def group_loads(G, last):
                s0 = W_FIRST + W_GROUP * G
                for h in range(GH):
                    load_chunk(s0 + h, (W_FIRST + h) % RAW, wo_src(G, h), False)
                if not last:
                    for k in range(6):
                        load_chunk(s0 + 4 + k, (W_FIRST + 4 + k) % RAW, chunk_src(k, G + 1), True)

            with sp.Fori(0, KVH - 1) as G:
                group_loads(G, False)
            group_loads(KVH - 1, True)

            for t in range(FFN_TILES):
                dst, s, _ = ffn_tile_src(t)
                if t < RAW:
                    sp.wait_ge(act_whi, W_FIRST + W_GROUP * KVH - 6 + t - RAW + 1)
                    sp.wait_ge(pool_wlo, W_FIRST + W_GROUP * KVH - 6 + t - RAW + 1)
                elif t == RAW:
                    sp.wait_ge(pe_block, BLOCKS - 4)
                elif t == RAW + 4:
                    sp.wait_ge(act_qhi, 4 * (UNITS - 1))
                    sp.wait_ge(dve_qlo, 2 * (UNITS - 1))
                    sp.wait_ge(pool_qlo, 2 * (UNITS - 1))
                src = w12[t * 128:(t + 1) * 128, :] if t < 8 else w3[(t - 8) * 128:(t - 7) * 128, :]
                sp.dma_start(dst, src).then_inc(s, 16)
            sp.wait_ge(act_khi, UNITS)
            sp.wait_ge(pool_klo, UNITS)
            sp.dma_start(b3_row[:, :], b3.partition_broadcast(128)).then_inc(bias3_loaded, 16)
            for b in range(B):
                sp.wait_ge(dve_out, b + 1)
                sp.dma_start(out[b], resid[:, b, :]).then_inc(out_stored, 16)
            sp.wait_ge(out_stored, 16 * B)

        @block.tensor
        def _(pe):
            def three(dst, st, mv_, start, stop):
                nc.tensor.matmul(dst, st[0], mv_[0], start=start, stop=False)
                nc.tensor.matmul(dst, st[0], mv_[1], start=False, stop=False)
                return nc.tensor.matmul(dst, st[1], mv_[0], start=False, stop=stop)

            def transpose4(dst, src):
                for t in range(4):
                    mm = nc.tensor.transpose(dst[:, t * 128:(t + 1) * 128], src(t), ident[:, :])
                return mm

            def tile(what, b):
                t = tile_of(what, b)
                before = t - 4 if t < len(TILES) - 4 else t - 2
                if before >= 0:
                    tiles_done(before)
                if what == "ctx":
                    pe.wait_ge(ctx_loaded[b], 16)
                    mm = transpose4(tile_bank(t), lambda k: ctx_raw[:, b, k * 128:(k + 1) * 128])
                elif what == "x":
                    pe.wait_ge(act_xn, b + 1)
                    mm = transpose4(tile_bank(t), lambda k: xnorm[:, b, k * 128:(k + 1) * 128])
                else:
                    pe.wait_ge(rope_loaded[2 * b], 16)
                    pe.wait_ge(rope_loaded[2 * b + 1], 16)
                    mm = transpose4(tile_bank(t), lambda k: rope_tok[:, 2 * b + k % 2, (k // 2) * 128:(k // 2 + 1) * 128])
                mm.then_inc(pe_tile, 1)

            def tiles_done(t):
                pe.wait_ge(act_tile, t + 1)
                pe.wait_ge(dve_tile, t + 1)

            def project(kind, half, bank, wready):
                pe.wait_ge(act_whi, wready)
                pe.wait_ge(pool_wlo, wready)
                hi, lo = chunk_dst(kind)
                mh, ml = (cT_hi, cT_lo) if kind < 2 else (xT_hi, xT_lo)
                for k in range(KT):
                    w = slice(k * 128, (k + 1) * 128)
                    tk = slice(half * HT, (half + 1) * HT)
                    mm = three(bank[:, :], (hi[:, w], lo[:, w]), (mh[:, k, tk], ml[:, k, tk]), k == 0, k == KT - 1)
                mm.then_inc(pe_block, 1)

            def bank_free(g, idx):
                p = idx - 2
                u2, j = 2 * g + p // 6, p % 6
                if j == 1:
                    pe.wait_ge(act_v32, u2 + 1)
                else:
                    pe.wait_ge(dve_rot, ropes_until(u2, j))

            def first_block(f):
                if f >= 2:
                    bank_free(0, f)
                project(f % 6, f // 6, f_bank[f % 2], f % 6 + 1)

            pe.wait_ge(ident_done, 1)
            for b in range(4):
                tile("ctx", b)
            tiles_done(tile_of("ctx", 3))
            first_block(0)
            tile("rope", 0)
            tile("rope", 1)
            first_block(1)
            for b in range(4):
                tile("x", b)
            pe.wait_ge(act_v32, 1)
            transpose4(pv_bank, lambda b: v32[:, b * 128:(b + 1) * 128]).then_inc(pe_vT, 1)
            tile("ctx", 4)
            tile("ctx", 5)
            tiles_done(tile_of("x", 3))
            first_block(2)
            tile("ctx", 6)
            tile("ctx", 7)
            first_block(3)
            first_block(4)
            first_block(5)
            tile("rope", 2)
            tile("rope", 3)
            tiles_done(tile_of("ctx", 7))
            first_block(6)

            def block_slot(g, c, i):
                idx = AHEAD + 3 * c + i
                if isinstance(g, int) and 12 * g + idx >= BLOCKS:
                    return
                bank_free(g, idx)
                G = g + idx // 12
                project(idx % 6, (idx // 6) % 2, f_bank[idx % 2], W_GROUP * G + idx % 6 + 1)

            def scores(g, c, k):
                n, sl = 8 * g + 2 * c + k, k
                u2, b = 2 * g + c // 2, 2 * (c % 2) + k
                pe.wait_ge(act_qhi, n + 1)
                pe.wait_ge(pool_qlo if k else dve_qlo, 4 * g + c + 1)
                if k == 0:
                    pe.wait_ge(act_khi, u2 + 1)
                    pe.wait_ge(pool_klo, u2 + 1)
                if not (isinstance(n, int) and n < 1):
                    pe.wait_ge(dve_masked, 2 * n)
                ks = (c // 2) % 2
                for h in range(GH):
                    nc.tensor.matmul(s_banks[:, 256 * h:256 * (h + 1)], q_hi[:, sl, h, :], k_parts[:, ks, b, :], start=True, stop=False)
                    mm = nc.tensor.matmul(s_banks[:, 256 * h:256 * h + 128], q_lo[:, sl, h, :], k_parts[:, ks, b, 0:128], start=False, stop=True)
                mm.then_inc(pe_score, 1)

            def prob_transpose(g, c, k):
                n = 8 * g + 2 * c + k
                pe.wait_ge(pool_norm, n + 1)
                pe.wait_ge(act_pThi, n)
                pe.wait_ge(dve_pTlo, n)
                transpose4(t_bank, lambda h: prob[:, k, h, :]).then_inc(pe_pT, 1)

            def pv(g, c, k):
                n = 8 * g + 2 * c + k
                u2, b = 2 * g + c // 2, 2 * (c % 2) + k
                pe.wait_ge(act_pThi, n + 1)
                pe.wait_ge(dve_pTlo, n + 1)
                done = u2 + 1 if last_unit(g, c) else u2 + 2
                pe.wait_ge(act_vhi, done)
                pe.wait_ge(dve_vlo, done)
                pe.wait_ge(act_ohi, n)
                pe.wait_ge(dve_olo, n)
                vs = (c // 2) % 2
                three(pv_bank[:, :], (v_hi[:, vs, b, :], v_lo[:, vs, b, :]),
                      (pT_hi[:, k].rearrange("p h s -> p (h s)"), pT_lo[:, k].rearrange("p h s -> p (h s)")), True, True).then_inc(pe_pv, 1)

            def out_proj(n, k, w_count):
                pe.wait_ge(act_ohi, n + 1)
                pe.wait_ge(dve_olo, n + 1)
                pe.wait_ge(act_whi, w_count)
                pe.wait_ge(pool_wlo, w_count)
                pe.wait_ge(dve_acc, n + 1)
                for h in range(GH):
                    mm = three(o_bank[k][:, :], (o_hi[:, k, h, :], o_lo[:, k, h, :]), (wo_hi[:, h, :], wo_lo[:, h, :]), h == 0, h == GH - 1)
                mm.then_inc(pe_out, 1)

            def pair(g, c):
                first = isinstance(g, int) and 4 * g + c == 0
                u_next = 2 * g + c // 2 + 1
                block_slot(g, c, 0)
                scores(g, c, 1)
                if c % 2 == 0:
                    if first:
                        pe.wait_ge(act_vhi, 1)
                        pe.wait_ge(dve_vlo, 1)
                    pe.wait_ge(act_v32, u_next + 1)
                    if not first:
                        pe.wait_ge(act_ohi, 8 * g + 2 * c)
                        pe.wait_ge(dve_olo, 8 * g + 2 * c)
                    transpose4(pv_bank, lambda b: v32[:, b * 128:(b + 1) * 128]).then_inc(pe_vT, 1)
                if first:
                    tile("x", 4)
                    tile("x", 5)
                else:
                    block_slot(g, c, 1)
                wcount = wo_count(g + (c - 1) // 4)
                prob_transpose(g, c, 0)
                if not first:
                    out_proj(8 * g + 2 * c - 2, 0, wcount)
                if first:
                    tile("x", 6)
                    tile("x", 7)
                pv(g, c, 0)
                prob_transpose(g, c, 1)
                if first:
                    tiles_done(tile_of("x", 7))
                    block_slot(g, c, 1)
                else:
                    out_proj(8 * g + 2 * c - 1, 1, wcount)
                pv(g, c, 1)
                scores(g, c + 1, 0)
                block_slot(g, c, 2)

            def wo_count(G):
                return W_FIRST + W_GROUP * G + GH

            def ffn_tile(t):
                src, loaded, count = ffn_tile_src(t)
                pe.wait_ge(loaded, count)
                if t < 2:
                    bank_free(KVH - 1, 12 + t)
                else:
                    pe.wait_ge(act_fstage, t - 1)
                transpose4(f_bank[t % 2], lambda k: src[:, k * 128:(k + 1) * 128]).then_inc(pe_ftile, 1)

            scores(0, 0, 0)
            pair(0, 0)
            with pe.Fori(0, KVH - 1) as g:
                for c in range(1, 5):
                    pair(g, c)
            pair(KVH - 1, 1)

            def h_tile(b):
                pe.wait_ge(act_xn, B + b + 1)
                if b < 2:
                    pe.wait_ge(act_fstage, 8 + (b == 0))
                elif b == 2:
                    pe.wait_ge(act_pThi, 8 * KVH)
                    pe.wait_ge(dve_pTlo, 8 * KVH)
                elif b == 3:
                    pe.wait_ge(act_ohi, 8 * KVH)
                    pe.wait_ge(dve_olo, 8 * KVH)
                elif b < 6:
                    pe.wait_ge(act_fstage, FFN_TILES)
                else:
                    tiles_done(H_T + b - 2)
                transpose4(h_bank(b), lambda k: xnorm2[:, b % 4, k * 128:(k + 1) * 128]).then_inc(pe_tile, 1)

            def up(half, m):
                i = 4 * half + m
                if i >= 2:
                    pe.wait_ge(dve_gate, i - 1)
                if i == 0:
                    pe.wait_ge(act_fhi, 8)
                    pe.wait_ge(pool_flo, 8)
                for part in range(2):
                    for k in range(KT):
                        w = slice((4 * part + m) * 128, (4 * part + m + 1) * 128)
                        tk = slice(half * HT, (half + 1) * HT)
                        mm = three(up_bank[2 * (i % 2) + part], (cT_hi[:, k, w], cT_lo[:, k, w]),
                                   (xT_hi[:, k, tk], xT_lo[:, k, tk]), k == 0, k == KT - 1)
                mm.then_inc(pe_up, 1)

            def down(half, b):
                n = 4 * half + b
                a_hi, a_lo = (wo_hi, wo_lo) if half == 0 else (act1_hi, act1_lo)
                if b == 0:
                    pe.wait_ge(act_ghi, 4 * (half + 1))
                    pe.wait_ge(dve_glo, 4 * (half + 1))
                if n == 0:
                    pe.wait_ge(dve_acc, 8 * KVH + 2)
                    pe.wait_ge(act_fhi, FFN_TILES)
                    pe.wait_ge(pool_flo, FFN_TILES)
                if n >= 2:
                    pe.wait_ge(dve_out, n - 1)
                for m in range(4):
                    ts = slice(b * 128, (b + 1) * 128)
                    mm = three(o_bank[n % 2][:, :], (a_hi[:, m, ts], a_lo[:, m, ts]), (wq_hi[:, m, :], wq_lo[:, m, :]), m == 0, m == 3)
                mm.then_inc(pe_down, 1)

            g, wcount = KVH - 1, wo_count(KVH - 1)
            n = 8 * KVH - 4
            ffn_tile(0)
            ffn_tile(1)
            out_proj(n - 2, 0, wcount)
            scores(g, 2, 1)
            ffn_tile(2)
            ffn_tile(3)
            prob_transpose(g, 2, 0)
            out_proj(n - 1, 1, wcount)
            pv(g, 2, 0)
            scores(g, 3, 0)
            prob_transpose(g, 2, 1)
            ffn_tile(4)
            out_proj(n, 0, wcount)
            pv(g, 2, 1)
            scores(g, 3, 1)
            ffn_tile(5)
            ffn_tile(6)
            prob_transpose(g, 3, 0)
            out_proj(n + 1, 1, wcount)
            pv(g, 3, 0)
            ffn_tile(7)
            prob_transpose(g, 3, 1)
            ffn_tile(8)
            out_proj(n + 2, 0, wcount)
            pv(g, 3, 1)

            for b in range(4):
                h_tile(b)
            out_proj(n + 3, 1, wcount)
            tiles_done(H_T + 1)
            ffn_tile(9)
            ffn_tile(10)
            tiles_done(H_T + 3)
            up(0, 0)
            ffn_tile(11)
            up(0, 1)
            h_tile(4)
            h_tile(5)
            up(0, 2)
            h_tile(6)
            h_tile(7)
            up(0, 3)
            tiles_done(H_T + 7)
            up(1, 0)
            up(1, 1)
            down(0, 0)
            down(0, 1)
            up(1, 2)
            up(1, 3)
            down(0, 2)
            down(0, 3)
            for b in range(4):
                down(1, b)

        def k4(bank):
            return bank.rearrange("p (k s) -> p k s", k=4)

        def ffn_tile_dst(t, part):
            if t < 8:
                return (cT_hi, cT_lo)[part][:, :, t * 128:(t + 1) * 128]
            return (wq_hi, wq_lo)[part][:, :, (t - 8) * 128:(t - 7) * 128]

        def ffn_stage(t):
            return (t_cos, t_sin)[t % 4 // 2][:, t % 2, :]

        @block.scalar
        def _(act):
            act.dma_start(pos_raw[:, :], pos.rearrange("b s -> s b"), allow_slow_non_contiguous=True).then_inc(pos_loaded, 16)
            act.dma_start(graw[:, 0:1], g_x.partition_broadcast(128)).then_inc(gate_loaded, 16)
            act.dma_start(graw[:, 1:2], g_f.partition_broadcast(128)).then_inc(gate_loaded, 16)
            act.dma_start(b12_col[:, :], b12.rearrange("(t p) -> p t", p=128), allow_slow_non_contiguous=True).then_inc(bias_loaded, 16)

            def hi(dst, src, s):
                nc.scalar.activation(dst, src, ACT.Copy).then_inc(s, 1)

            act.wait_ge(gate_loaded, 32)
            nc.scalar.activation(small[:, 24:26], graw, ACT.Tanh).then_inc(act_small, 1)

            def tile_copy(what, b):
                t = tile_of(what, b)
                act.wait_ge(pe_tile, t + 1)
                if what == "rope":
                    hi(cosT[:, b * 256:(b + 1) * 256], tile_bank(t)[:, 0:256], act_tile)
                else:
                    dst = cT_hi if what == "ctx" else xT_hi
                    hi(dst[:, :, b * 128:(b + 1) * 128], k4(tile_bank(t)), act_tile)

            def split_chunk(done, slot, loaded, dst, free):
                act.wait_ge(raw_loaded[slot], loaded)
                if free is not None:
                    act.wait_ge(*free)
                hi(dst[0], raw[:, slot, :], act_whi)

            def first_chunk(s):
                split_chunk(s + 1, s % RAW, 16 * (s // RAW + 1), chunk_dst(s), None)

            def exps(g, c, k):
                n = 8 * g + 2 * c + k
                act.wait_ge(dve_mask, n + 1)
                for h in range(GH):
                    e = nc.scalar.activation(prob[:, k, h, :], prob[:, k, h, :], ACT.Exp, bias=nmin[k][:, h:h + 1],
                                             scale=-1.0, accum_out=psum_row[k][:, h:h + 1])
                e.then_inc(act_exp, 1)

            def v_copy(g, c):
                u2 = 2 * g + c // 2 + 1
                act.wait_ge(pe_block, 6 * u2 + 2)
                act.wait_ge(pe_vT, u2)
                hi(v32[:, :], f_bank[1][:, :], act_v32)

            def v_hi_copy(u2, vs):
                act.wait_ge(pe_vT, u2 + 1)
                if not (isinstance(u2, int) and u2 < 2):
                    act.wait_ge(pe_pv, 4 * u2 - 4)
                hi(v_hi[:, vs], k4(pv_bank[:, :]), act_vhi)

            def k_hi_copy(u2, ks):
                act.wait_ge(pool_rope, ropes_until(u2, 0))
                if not (isinstance(u2, int) and u2 < 2):
                    act.wait_ge(pe_score, 4 * u2 - 4)
                hi(k_parts[:, ks, :, 0:S], k4(k32[:, :]), act_khi)

            def q_hi_copy(n, u2, qs, k, b):
                act.wait_ge(pool_rope, 5 * u2 + 5)
                if not (isinstance(n, int) and n < 2):
                    act.wait_ge(pe_score, n - 1)
                hi(q_hi[:, k], q32[:, qs, :, b * S:(b + 1) * S], act_qhi)

            def pT_hi_copy(g, c, k):
                n = 8 * g + 2 * c + k
                act.wait_ge(pe_pT, n + 1)
                if not (isinstance(n, int) and n < 2):
                    act.wait_ge(pe_pv, n - 1)
                hi(pT_hi[:, k], k4(t_bank[:, :]), act_pThi)

            def o_hi_copy(g, c, k):
                n = 8 * g + 2 * c + k
                act.wait_ge(pe_pv, n + 1)
                if not (isinstance(n, int) and n < 2):
                    act.wait_ge(pe_out, n - 1)
                hi(o_hi[:, k], k4(pv_bank[:, :]), act_ohi)

            def normalise(dst, b):
                nc.scalar.activation(dst, resid[:, b, :], ACT.Identity, bias=shift[:, b:b + 1], scale=rstd[:, b:b + 1]).then_inc(act_xn, 1)

            def x_norms(half):
                act.wait_ge(dve_shift, half + 1)
                for b in range(4 * half, 4 * half + 4):
                    normalise(xnorm[:, b, :], b)

            tile_copy("ctx", 0)
            tile_copy("ctx", 1)
            first_chunk(0)
            tile_copy("ctx", 2)
            tile_copy("ctx", 3)
            for s in range(1, 5):
                first_chunk(s)
            tile_copy("rope", 0)
            tile_copy("rope", 1)
            x_norms(0)
            act.wait_ge(pe_block, 2)
            hi(v32[:, :], f_bank[1][:, :], act_v32)
            for b in range(4):
                tile_copy("x", b)
            v_hi_copy(0, 0)
            tile_copy("ctx", 4)
            tile_copy("ctx", 5)
            k_hi_copy(0, 0)
            first_chunk(5)
            tile_copy("ctx", 6)
            tile_copy("ctx", 7)
            tile_copy("rope", 2)
            tile_copy("rope", 3)
            q_hi_copy(0, 0, 0, 0, 0)
            q_hi_copy(1, 0, 0, 1, 1)
            x_norms(1)

            def ffn_tile_copy(t):
                act.wait_ge(pe_ftile, t + 1)
                if t < 2:
                    act.wait_ge(pool_rope, 5 * UNITS)
                elif t >= 4:
                    act.wait_ge(pool_flo, t - 3)
                hi(ffn_stage(t), f_bank[t % 2][:, :], act_fstage)
                act.wait_ge(act_fstage, t + 1)
                hi(ffn_tile_dst(t, 0), k4(ffn_stage(t)), act_fhi)

            def pair(g, c):
                u2 = 2 * g + c // 2
                chunks = pair_chunks(g, c)
                exps(g, c, 0)
                if c % 4:
                    for ch in chunks[:1]:
                        split_chunk(*ch)
                if c % 2 == 0:
                    v_copy(g, c)
                    v_hi_copy(u2 + 1, (c // 2 + 1) % 2)
                    k_hi_copy(u2 + 1, (c // 2 + 1) % 2)
                elif c % 4:
                    for ch in chunks[1:2]:
                        split_chunk(*ch)
                first = isinstance(g, int) and 4 * g + c == 0
                if first:
                    tile_copy("x", 4)
                    tile_copy("x", 5)
                exps(g, c, 1)
                pT_hi_copy(g, c, 0)
                if first:
                    tile_copy("x", 6)
                    tile_copy("x", 7)
                if c % 4:
                    for ch in chunks[2 if c % 2 else 1:]:
                        split_chunk(*ch)
                o_hi_copy(g, c, 0)
                pT_hi_copy(g, c, 1)
                next_queries(g, c)
                o_hi_copy(g, c, 1)
                if c % 4 == 0:
                    for ch in chunks:
                        split_chunk(*ch)

            def next_queries(g, c):
                for k in range(2):
                    q_hi_copy(8 * g + 2 * c + 2 + k, 2 * g + (c + 1) // 2, ((c + 1) // 2) % 2, k, 2 * ((c + 1) % 2) + k)

            pair(0, 0)
            with act.Fori(0, KVH - 1) as g:
                for c in range(1, 5):
                    pair(g, c)
            pair(KVH - 1, 1)
            g = KVH - 1
            ffn_tile_copy(0)
            ffn_tile_copy(1)
            exps(g, 2, 0)
            next_queries(g, 2)
            pT_hi_copy(g, 2, 0)
            exps(g, 2, 1)
            ffn_tile_copy(2)
            o_hi_copy(g, 2, 0)
            ffn_tile_copy(3)
            pT_hi_copy(g, 2, 1)
            ffn_tile_copy(4)
            exps(g, 3, 0)
            o_hi_copy(g, 2, 1)
            ffn_tile_copy(5)
            pT_hi_copy(g, 3, 0)
            exps(g, 3, 1)
            ffn_tile_copy(6)
            o_hi_copy(g, 3, 0)
            ffn_tile_copy(7)
            pT_hi_copy(g, 3, 1)
            ffn_tile_copy(8)
            def h_norm(b):
                act.wait_ge(dve_shift, 3 + b // 4)
                if b >= 4:
                    act.wait_ge(pe_tile, H_T + b - 4 + 1)
                normalise(xnorm2[:, b % 4, :], b)

            def h_copy(b):
                act.wait_ge(pe_tile, H_T + b + 1)
                hi(xT_hi[:, :, b * 128:(b + 1) * 128], k4(h_bank(b)[:, :]), act_tile)

            def gate(half, m):
                i = 4 * half + m
                a_hi = wo_hi if half == 0 else act1_hi
                act.wait_ge(pe_up, i + 1)
                if i < 2:
                    act.wait_ge(pool_flo, FFN_TILES - 1 + i)
                else:
                    act.wait_ge(dve_gate, i - 1)
                nc.scalar.activation(t_cos[:, i % 2, :], up_bank[2 * (i % 2)], ACT.Silu, bias=b12_col[:, m:m + 1]).then_inc(act_silu, 1)
                act.wait_ge(dve_gate, i + 1)
                if i == 0:
                    act.wait_ge(pe_out, 8 * KVH)
                hi(a_hi[:, m, :], t_sin[:, i % 2, :], act_ghi)

            h_norm(0)
            h_norm(1)
            o_hi_copy(g, 3, 1)
            h_norm(2)
            h_norm(3)
            for b in range(4):
                h_copy(b)
            ffn_tile_copy(9)
            ffn_tile_copy(10)
            h_norm(4)
            h_norm(5)
            ffn_tile_copy(11)
            act.wait_ge(bias_loaded, 16)
            gate(0, 0)
            h_norm(6)
            h_norm(7)
            h_copy(4)
            h_copy(5)
            gate(0, 1)
            h_copy(6)
            h_copy(7)
            gate(0, 2)
            gate(0, 3)
            for m in range(4):
                gate(1, m)

        @block.gpsimd
        def _(pool):
            pool.memset(ident[:, :], 0.0).then_inc(ident_zero, 1)
            pool.wait_ge(ident_zero, 1)
            pool.affine_select(out=ident[:, :], in_=ident[:, :], compare_op=ALU.not_equal, fill=1.0, base=0,
                               pattern=[[-1, 128]], channel_multiplier=1).then_inc(ident_done, 1)
            pool.wait_ge(dve_small, 3)

            def gather(b):
                pool.indirect_dma_start(rope_tok[:, b, :], None, table[:, :],
                                        bass.IndirectOffsetOnAxis(ap=pos_fix[:, b:b + 1], axis=0)).then_inc(rope_loaded[b], 16)

            def minus(dst, a, b_, s):
                nc.gpsimd.tensor_tensor(dst, a, b_, ALU.subtract).then_inc(s, 1)

            def split_chunk(done, slot, loaded, dst, free):
                pool.wait_ge(act_whi, done)
                minus(dst[1], raw[:, slot, :], f32(dst[0]), pool_wlo)


            def rope_add(g, idx):
                u2, j = 2 * g + idx // 6, idx % 6
                cnt = ropes_until(u2, j)
                ts = rope_slot(idx)
                pool.wait_ge(dve_rot, cnt)
                fixed = isinstance(g, int)
                if j == 0:
                    if not (fixed and 12 * g + idx < 6):
                        pool.wait_ge(act_khi, u2)
                        pool.wait_ge(pool_klo, u2)
                    dst = k32[:, :]
                else:
                    if not (fixed and 12 * g + idx < 12):
                        pool.wait_ge(act_qhi, 4 * u2 - 4)
                        pool.wait_ge(dve_qlo, 2 * u2 - 2)
                        pool.wait_ge(pool_qlo, 2 * u2 - 2)
                    dst = q32[:, (idx // 6) % 2, j - 2, :]
                nc.gpsimd.tensor_tensor(dst, t_cos[:, ts, :], t_sin[:, ts, :], ALU.add).then_inc(pool_rope, 1)

            def k_lo_split(u2, ks):
                pool.wait_ge(act_khi, u2 + 1)
                minus(k_parts[:, ks, :, S:2 * S], k4(k32[:, :]), f32(k_parts[:, ks, :, 0:S]), pool_klo)

            def q_lo_split(g, c):
                b = 2 * (c % 2) + 1
                pool.wait_ge(act_qhi, 8 * g + 2 * c + 2)
                minus(q_lo[:, 1], q32[:, (c // 2) % 2, :, b * S:(b + 1) * S], f32(q_hi[:, 1]), pool_qlo)

            def norm(g, c, k):
                n = 8 * g + 2 * c + k
                pool.wait_ge(dve_recip, n + 1)
                nc.gpsimd.tensor_tensor(prob[:, k], prob[:, k], rrow[k].unsqueeze(2).to_broadcast([128, GH, S]), ALU.mult).then_inc(pool_norm, 1)

            def first_chunk(s):
                split_chunk(s + 1, s % RAW, None, chunk_dst(s), None)

            for b in range(4):
                gather(b)
            for s in range(5):
                first_chunk(s)
            rope_add(0, 0)
            k_lo_split(0, 0)
            first_chunk(5)
            for b in range(4, 8):
                gather(b)
            for f in range(2, 6):
                rope_add(0, f)
            q_lo_split(0, 0)
            def pair(g, c):
                u2 = 2 * g + c // 2
                idx = AHEAD + 3 * c
                chunks = pair_chunks(g, c)
                rope_add(g, idx - 1)
                norm(g, c, 0)
                if c % 2 == 0:
                    k_lo_split(u2 + 1, (c // 2 + 1) % 2)
                early = 2 if c % 2 else 1
                if c % 4:
                    for ch in chunks[:early]:
                        split_chunk(*ch)
                norm(g, c, 1)
                if c % 2:
                    rope_add(g, idx)
                    rope_add(g, idx + 1)
                    q_lo_split(g, c + 1)
                if c % 4:
                    for ch in chunks[early:]:
                        split_chunk(*ch)
                if c % 2 == 0:
                    q_lo_split(g, c + 1)
                    rope_add(g, idx + 1)
                if c % 4 == 0:
                    for ch in chunks:
                        split_chunk(*ch)

            pair(0, 0)
            with pool.Fori(0, KVH - 1) as g:
                for c in range(1, 5):
                    pair(g, c)
            pair(KVH - 1, 1)

            def ffn_tile_lo(t):
                pool.wait_ge(act_fhi, t + 1)
                minus(ffn_tile_dst(t, 1), k4(ffn_stage(t)), f32(ffn_tile_dst(t, 0)), pool_flo)

            g = KVH - 1
            ffn_tile_lo(0)
            ffn_tile_lo(1)
            norm(g, 2, 0)
            q_lo_split(g, 3)
            norm(g, 2, 1)
            for t in range(2, 5):
                ffn_tile_lo(t)
            norm(g, 3, 0)
            ffn_tile_lo(5)
            norm(g, 3, 1)
            for t in range(6, FFN_TILES):
                ffn_tile_lo(t)

        @block.vector
        def _(dve):
            dve.sem_inc(dve_acc, 2)
            dve.wait_ge(pos_loaded, 16)
            nc.vector.tensor_scalar(posf, pos_raw[:, :], 0.0, float(MAX_POS), ALU.is_lt, ALU.mult).then_inc(dve_small, 1)
            dve.wait_ge(dve_small, 1)
            nc.vector.tensor_tensor(posf, posf, pos_raw[:, :], ALU.add).then_inc(dve_small, 1)
            dve.wait_ge(dve_small, 2)
            nc.vector.tensor_scalar(pos_fix[:, :], posf, 0.0, float(MAX_POS - 1), ALU.max, ALU.min).then_inc(dve_small, 1)

            def lo(dst, src, hi_part, s):
                nc.vector.tensor_tensor(dst, src, f32(hi_part), ALU.subtract).then_inc(s, 1)

            def stats_of(b, s_cnt):
                nc.vector.bn_stats(stats, resid[:, b, :]).then_inc(dve_st, 1)
                dve.wait_ge(dve_st, s_cnt + 1)
                nc.vector.bn_aggr(mv[:, b, :], stats).then_inc(dve_st, 1)
                dve.wait_ge(dve_st, s_cnt + 2)

            def inv_std(b0, b1, done):
                v, y, t = var[:, b0:b1], rstd[:, b0:b1], newton[:, b0:b1]

                def after(op):
                    nonlocal done
                    op.then_inc(dve_newton, 1)
                    done += 1
                    dve.wait_ge(dve_newton, done)
                after(nc.vector.tensor_scalar(v, mv[:, b0:b1, 1], EPS, None, ALU.add))
                after(nc.vector.tensor_scalar(y.bitcast(I32), v.bitcast(I32), -0.5, float(0x5F3759DF), ALU.mult, ALU.add))
                for _ in range(NEWTON):
                    after(nc.vector.scalar_tensor_tensor(out=t, in0=y, scalar=-0.5, in1=y, op0=ALU.mult, op1=ALU.mult))
                    after(nc.vector.tensor_tensor(t, t, v, ALU.mult))
                    after(nc.vector.scalar_tensor_tensor(out=y, in0=t, scalar=1.5, in1=y, op0=ALU.add, op1=ALU.mult))

            def shifts(b0, b1):
                nc.vector.scalar_tensor_tensor(out=shift[:, b0:b1], in0=mv[:, b0:b1, 0], scalar=-1.0, in1=rstd[:, b0:b1],
                                               op0=ALU.mult, op1=ALU.mult).then_inc(dve_shift, 1)

            def tile_lo(what, b):
                t = tile_of(what, b)
                bank = tile_bank(t)
                dve.wait_ge(act_tile, t + 1)
                if what == "rope":
                    nc.vector.tensor_copy(sinT[:, b * 256:(b + 1) * 256], bank[:, 256:512]).then_inc(dve_tile, 1)
                else:
                    dst, h = (cT_lo, cT_hi) if what == "ctx" else (xT_lo, xT_hi)
                    sl = slice(b * 128, (b + 1) * 128)
                    lo(dst[:, :, sl], k4(bank), h[:, :, sl], dve_tile)

            def x_stats(b):
                dve.wait_ge(x_loaded[b], 16)
                stats_of(b, 2 * b)

            def rotate(g, idx):
                u2, j, half = 2 * g + idx // 6, idx % 6, (idx // 6) % 2
                fixed = isinstance(g, int)
                bank = f_bank[idx % 2]
                ts = rope_slot(idx)
                f_cnt = 12 * g + idx + 1
                dve.wait_ge(pe_block, f_cnt)
                cnt = ropes_until(u2, j)
                if not (fixed and ropes_until(2 * g + idx // 6, j) <= 2):
                    dve.wait_ge(pool_rope, cnt - 2)
                if fixed and 12 * g + idx in (0, 6):
                    dve.wait_ge(act_tile, tile_of("rope", 2 * half + 1) + 1)
                    dve.wait_ge(dve_tile, tile_of("rope", 2 * half + 1) + 1)
                tk = slice(half * HT, (half + 1) * HT)

                def times(dst, a, b_):
                    if j == 0:
                        return nc.vector.scalar_tensor_tensor(out=dst, in0=a, scalar=SCORE_SCALE, in1=b_, op0=ALU.mult, op1=ALU.mult)
                    return nc.vector.tensor_tensor(dst, a, b_, ALU.mult)
                times(t_cos[:, ts, :], bank[:, :], cosT[:, tk])
                times(t_sin[64:128, ts, :], bank[0:64, :], sinT[0:64, tk])
                times(t_sin[0:64, ts, :], bank[64:128, :], sinT[64:128, tk]).then_inc(dve_rot, 1)

            def v_lo_split(u2, vs):
                dve.wait_ge(act_vhi, u2 + 1)
                lo(v_lo[:, vs], k4(pv_bank[:, :]), v_hi[:, vs], dve_vlo)

            for b in range(4):
                tile_lo("ctx", b)
            for b in range(4):
                x_stats(b)
            inv_std(0, 4, 0)
            shifts(0, 4)
            tile_lo("rope", 0)
            tile_lo("rope", 1)
            rotate(0, 0)
            for b in range(4):
                tile_lo("x", b)
            v_lo_split(0, 0)
            x_stats(4)
            x_stats(5)
            x_stats(6)
            x_stats(7)
            rotate(0, 2)
            tile_lo("ctx", 4)
            tile_lo("ctx", 5)
            rotate(0, 3)
            tile_lo("ctx", 6)
            tile_lo("ctx", 7)
            rotate(0, 4)
            rotate(0, 5)
            inv_std(4, 8, NEWTON_OPS)
            shifts(4, 8)

            def q_lo_split(g, c):
                b = 2 * (c % 2)
                dve.wait_ge(act_qhi, 8 * g + 2 * c + 1)
                lo(q_lo[:, 0], q32[:, (c // 2) % 2, :, b * S:(b + 1) * S], q_hi[:, 0], dve_qlo)

            def mask_scores(g, c, k):
                n = 8 * g + 2 * c + k
                dve.wait_ge(pe_score, n + 1)
                if not (isinstance(n, int) and n < 2):
                    dve.wait_ge(pe_pT, n - 1)
                b = (2 * c + k) % B
                if first_step(n):
                    dve.wait_ge(dve_small, 4)
                nc.vector.tensor_tensor(prob[:, k], s_parts[:, :, 1, :], mfill[:, b, :].unsqueeze(1).to_broadcast([128, GH, S]),
                                        ALU.add).then_inc(dve_masked, 1)
                dve.wait_ge(dve_masked, 2 * n + 1)
                nc.vector.tensor_tensor(prob[:, k], s_parts[:, :, 0, :], prob[:, k], ALU.add).then_inc(dve_masked, 1)
                dve.wait_ge(dve_masked, 2 * n + 2)
                nc.vector.tensor_reduce(nmin[k], prob[:, k], mybir.AxisListType.X, ALU.min).then_inc(dve_mask, 1)

            def first_step(n):
                return isinstance(n, int) and n == 0

            def recip(g, c, k):
                dve.wait_ge(act_exp, 8 * g + 2 * c + k + 1)
                nc.vector.reciprocal(rrow[k], psum_row[k]).then_inc(dve_recip, 1)

            def pT_lo_split(g, c, k):
                dve.wait_ge(act_pThi, 8 * g + 2 * c + k + 1)
                lo(pT_lo[:, k], k4(t_bank[:, :]), pT_hi[:, k], dve_pTlo)

            def o_lo_split(g, c, k):
                dve.wait_ge(act_ohi, 8 * g + 2 * c + k + 1)
                lo(o_lo[:, k], k4(pv_bank[:, :]), o_hi[:, k], dve_olo)

            def add_out(n, b, k):
                dve.wait_ge(pe_out, n + 1)
                nc.vector.scalar_tensor_tensor(out=resid[:, b, :], in0=o_bank[k][:, :], scalar=tg_x, in1=resid[:, b, :],
                                               op0=ALU.mult, op1=ALU.add).then_inc(dve_acc, 1)

            def pair(g, c):
                u2 = 2 * g + c // 2
                idx = AHEAD + 3 * c
                first = isinstance(g, int) and 4 * g + c == 0
                rotate(g, idx - 1)
                recip(g, c, 0)
                mask_scores(g, c, 1)
                if c % 2:
                    rotate(g, idx)
                    recip(g, c, 1)
                    pT_lo_split(g, c, 0)
                    rotate(g, idx + 1)
                else:
                    v_lo_split(u2 + 1, (c // 2 + 1) % 2)
                    if first:
                        tile_lo("x", 4)
                        tile_lo("x", 5)
                    else:
                        rotate(g, idx + 1)
                    recip(g, c, 1)
                    pT_lo_split(g, c, 0)
                if first:
                    tile_lo("x", 6)
                    tile_lo("x", 7)
                else:
                    add_out(8 * g + 2 * c - 2, (2 * c - 2) % B, 0)
                o_lo_split(g, c, 0)
                pT_lo_split(g, c, 1)
                q_lo_split(g, c + 1)
                if first:
                    rotate(g, idx + 1)
                else:
                    add_out(8 * g + 2 * c - 1, (2 * c - 1) % B, 1)
                o_lo_split(g, c, 1)
                mask_scores(g, c + 1, 0)

            def h_stats(b):
                dve.wait_ge(dve_acc, 2 + 8 * (KVH - 1) + b + 1)
                stats_of(b, 2 * B + 2 * b)

            def h_lo(b):
                dve.wait_ge(act_tile, H_T + b + 1)
                sl = slice(b * 128, (b + 1) * 128)
                lo(xT_lo[:, :, sl], k4(h_bank(b)[:, :]), xT_hi[:, :, sl], dve_tile)

            dve.wait_ge(act_small, 1)
            q_lo_split(0, 0)
            tile_lo("rope", 2)
            tile_lo("rope", 3)
            dve.wait_ge(mask_loaded, 16)
            nc.vector.tensor_scalar(mfill[:, :, :], mask_raw[:, :, :], 0.0, MASKED, ALU.is_equal, ALU.mult).then_inc(dve_small, 1)
            mask_scores(0, 0, 0)
            pair(0, 0)
            with dve.Fori(0, KVH - 1) as g:
                for c in range(1, 5):
                    pair(g, c)
            pair(KVH - 1, 1)
            g = KVH - 1
            n = 8 * KVH - 4
            h_stats(0)
            add_out(n - 2, 2, 0)
            recip(g, 2, 0)
            mask_scores(g, 2, 1)
            q_lo_split(g, 3)
            pT_lo_split(g, 2, 0)
            recip(g, 2, 1)
            h_stats(1)
            add_out(n - 1, 3, 1)
            o_lo_split(g, 2, 0)
            mask_scores(g, 3, 0)
            pT_lo_split(g, 2, 1)
            h_stats(2)
            add_out(n, 4, 0)
            recip(g, 3, 0)
            o_lo_split(g, 2, 1)
            mask_scores(g, 3, 1)
            pT_lo_split(g, 3, 0)
            h_stats(3)
            recip(g, 3, 1)
            add_out(n + 1, 5, 1)
            o_lo_split(g, 3, 0)
            inv_std(0, 4, 2 * NEWTON_OPS)
            shifts(0, 4)
            pT_lo_split(g, 3, 1)
            h_stats(4)
            add_out(n + 2, 6, 0)
            o_lo_split(g, 3, 1)

            h_lo(0)
            h_lo(1)
            h_stats(5)
            h_lo(2)
            h_lo(3)
            h_stats(6)
            add_out(n + 3, 7, 1)
            h_stats(7)
            inv_std(4, 8, 3 * NEWTON_OPS)
            shifts(4, 8)
            dve.wait_ge(bias3_loaded, 16)

            def gate(half, m):
                i = 4 * half + m
                a_hi, a_lo = (wo_hi, wo_lo) if half == 0 else (act1_hi, act1_lo)
                dve.wait_ge(act_silu, i + 1)
                if i >= 2:
                    dve.wait_ge(act_ghi, i - 1)
                    dve.wait_ge(dve_glo, i - 1)
                nc.vector.scalar_tensor_tensor(out=t_sin[:, i % 2, :], in0=up_bank[2 * (i % 2) + 1], scalar=b12_col[:, 4 + m:5 + m],
                                               in1=t_cos[:, i % 2, :], op0=ALU.add, op1=ALU.mult).then_inc(dve_gate, 1)
                dve.wait_ge(act_ghi, i + 1)
                lo(a_lo[:, m, :], t_sin[:, i % 2, :], a_hi[:, m, :], dve_glo)
                nc.vector.scalar_tensor_tensor(out=resid[:, i, :], in0=b3_row[:, :], scalar=tg_f, in1=resid[:, i, :],
                                               op0=ALU.mult, op1=ALU.add).then_inc(dve_b3, 1)

            def result(n):
                dve.wait_ge(pe_down, n + 1)
                dve.wait_ge(dve_b3, n + 1)
                nc.vector.scalar_tensor_tensor(out=resid[:, n, :], in0=o_bank[n % 2][:, :], scalar=tg_f, in1=resid[:, n, :],
                                               op0=ALU.mult, op1=ALU.add).then_inc(dve_out, 1)

            gate(0, 0)
            h_lo(4)
            h_lo(5)
            gate(0, 1)
            h_lo(6)
            h_lo(7)
            gate(0, 2)
            gate(0, 3)
            gate(1, 0)
            gate(1, 1)
            result(0)
            result(1)
            gate(1, 2)
            gate(1, 3)
            for n in range(2, 8):
                result(n)


_INS = ['x', 'ctx_4096', 'pos_BxS2', 'mask_BxSxS2_ik0', 'g_xattn', 'g_ffn', 'L0_xattn_Wq', 'L0_xattn_Wk', 'L0_xattn_Wv',
        'L0_xattn_Wo', 'L0_ffn_w12', 'L0_ffn_b12', 'L0_ffn_w3', 'L0_ffn_b3']
_OUTS = [((8, 128, 512), 'float32')]


def kernel(**inputs):
    import numpy as _np
    import concourse.bacc as _bacc
    from concourse import mybir as _mybir
    from concourse.bass_utils import run_bass_kernel_spmd as _run

    nc = _bacc.Bacc("TRN2", target_bir_lowering=False, num_devices=1, dynamic_dma_scratch_size=4096)
    arrays, args = {}, []
    for name in _INS:
        a = _np.ascontiguousarray(inputs[name])
        arrays[f"in_{name}_dram"] = a
        args.append(nc.dram_tensor(f"in_{name}_dram", a.shape, _mybir.dt.from_np(a.dtype), kind="ExternalInput").ap())
    for i, (shape, dtype) in enumerate(_OUTS):
        dt = _mybir.dt.from_np(_np.dtype(dtype))
        args.append(nc.dram_tensor(f"out_{i}_dram", shape, dt, kind="ExternalOutput").ap())
    build(nc, *args)
    r = _run(nc, [arrays], core_ids=[0])
    return r.results[0]["out_0_dram"]
```
